# Optimizing a Trainium2 kernel written in Bass

```python
import numpy as np
import jax
import jax.numpy as jnp

def _softmax(x, axis=-1):
    return jax.nn.softmax(x, axis=axis)

def _gelu(x):
    return jax.nn.gelu(x, approximate=True)

def _silu(x):
    return jax.nn.silu(x)

def _sigmoid(x):
    return jax.nn.sigmoid(x)

def _layernorm(x, axis=-1, eps=1e-05):
    m = jnp.mean(x, axis=axis, keepdims=True)
    v = jnp.var(x, axis=axis, keepdims=True)
    return (x - m) / jnp.sqrt(v + eps)

def _scatter_add(tgt, idx, src, axis=0):
    return tgt.at[idx].add(src)

def _segment_sum(src, seg, n):
    return jax.ops.segment_sum(src, seg, n)
kernel_name = 'mk_conv_preact_d1_conv_nchw512_r2_c320a2'

def setup_inputs(seed: int=0):
    np.random.seed(seed)
    _w = jnp.asarray

    def _rec_inputs():
        import jax
        import jax.numpy as jnp
        _gk = jax.random.key(seed)
        x = -9.26e-05 + 0.9999 * jax.random.normal(jax.random.fold_in(_gk, 1), (32, 256, 48, 48), jnp.float32)
        return x
    x = _rec_inputs()

    def _L0_conv_setup():
        import jax, jax.numpy as jnp
        import numpy as np
        K = 3
        M = 4
        key = jax.random.key(seed)
        ks = jax.random.split(key, 10)
        N, C, H, W = (32, 256, 48, 48)
        Cm = C // M
        P = 256
        sc = 0.05
        x = jax.random.normal(ks[0], (N, C, H, W), jnp.float32)
        Wc = jax.random.normal(ks[1], (Cm, C), jnp.float32) * sc
        bc = jax.random.normal(ks[2], (Cm,), jnp.float32) * sc
        Wkk = jax.random.normal(ks[3], (K * K,), jnp.float32) * sc
        bkk = jax.random.normal(ks[4], (K * K,), jnp.float32) * sc
        Wck = jax.random.normal(ks[5], (Cm, 2), jnp.float32) * sc
        bck = jax.random.normal(ks[6], (Cm,), jnp.float32) * sc
        b_ad = jax.random.normal(ks[7], (Cm,), jnp.float32) * sc
        Wf = jax.random.normal(ks[8], (P, Cm), jnp.float32) * sc
        bf = jax.random.normal(ks[9], (P,), jnp.float32) * sc
        return {'x': x, 'Wc': Wc, 'bc': bc, 'Wkk': Wkk, 'bkk': bkk, 'Wck': Wck, 'bck': bck, 'b_ad': b_ad, 'Wf': Wf, 'bf': bf}
    _L0_conv_all = _L0_conv_setup()
    _L0_conv_in = {k: v for k, v in _L0_conv_all.items() if k in ('Wc', 'bc', 'Wkk', 'bkk', 'Wck', 'bck', 'b_ad', 'Wf', 'bf')}
    del _L0_conv_all
    return {'x': x, 'L0_conv_Wc': _L0_conv_in['Wc'], 'L0_conv_bc': _L0_conv_in['bc'], 'L0_conv_Wkk': _L0_conv_in['Wkk'], 'L0_conv_bkk': _L0_conv_in['bkk'], 'L0_conv_Wck': _L0_conv_in['Wck'], 'L0_conv_bck': _L0_conv_in['bck'], 'L0_conv_b_ad': _L0_conv_in['b_ad'], 'L0_conv_Wf': _L0_conv_in['Wf'], 'L0_conv_bf': _L0_conv_in['bf']}

def reference(x, L0_conv_Wc, L0_conv_bc, L0_conv_Wkk, L0_conv_bkk, L0_conv_Wck, L0_conv_bck, L0_conv_b_ad, L0_conv_Wf, L0_conv_bf):
    import jax
    import jax.numpy as jnp

    def _L0_conv_ref(x, Wc, bc, Wkk, bkk, Wck, bck, b_ad, Wf, bf):
        import jax, jax.numpy as jnp
        import numpy as np
        K = 3
        M = 4
        N, C, H, W = x.shape
        Cm = Wc.shape[0]
        k = K
        pad = (k - 1) // 2
        f = jax.nn.relu(jnp.einsum('oc,nchw->nohw', Wc, x) + bc[None, :, None, None])
        gk1 = jax.nn.relu(jnp.mean(x, axis=(2, 3)) @ Wc.T + bc)
        g_kern = (gk1[:, :, None] * Wkk[None, None, :] + bkk[None, None, :]).reshape(N, Cm, k, k)
        xm = x.reshape(N, C, k, H // k, k, W // k).max(axis=(3, 5))
        sk = jax.nn.relu(jnp.einsum('oc,nckl->nokl', Wc, xm) + bc[None, :, None, None])
        gs = jnp.stack([g_kern, sk], axis=2)
        dynW = jax.nn.relu(jnp.einsum('oj,ncjkl->nockl', Wck, gs) + bck[None, :, None, None, None])

        def conv_one(fn, wn):
            return jax.lax.conv_general_dilated(fn[None], wn, window_strides=(1, 1), padding=[(pad, pad), (pad, pad)])[0]
        y = jax.vmap(conv_one)(f, dynW) + b_ad[None, :, None, None]
        out = jnp.einsum('oc,nchw->nohw', Wf, y) + bf[None, :, None, None]
        return out

    def _gn(v, G=32, eps=1e-05):
        B_, C_, H_, W_ = v.shape
        g = v.reshape(B_, G, C_ // G, H_, W_)
        m = jnp.mean(g, axis=(2, 3, 4), keepdims=True)
        s = jnp.var(g, axis=(2, 3, 4), keepdims=True)
        return ((g - m) / jnp.sqrt(s + eps)).reshape(v.shape)

    def _ln_c(v, eps=1e-06):
        m = jnp.mean(v, axis=1, keepdims=True)
        s = jnp.var(v, axis=1, keepdims=True)
        return (v - m) / jnp.sqrt(s + eps)

    def _ln_t(v, eps=1e-05):
        m = jnp.mean(v, axis=-1, keepdims=True)
        s = jnp.var(v, axis=-1, keepdims=True)
        return (v - m) / jnp.sqrt(s + eps)

    def _to_tokens(v):
        B_, C_, H_, W_ = v.shape
        return v.reshape(B_, C_, H_ * W_).transpose(0, 2, 1)

    def _from_tokens(t, like):
        B_, C_, H_, W_ = like.shape
        return t.transpose(0, 2, 1).reshape(B_, C_, H_, W_)
    x = x + _L0_conv_ref(_gn(x), L0_conv_Wc, L0_conv_bc, L0_conv_Wkk, L0_conv_bkk, L0_conv_Wck, L0_conv_bck, L0_conv_b_ad, L0_conv_Wf, L0_conv_bf)
    return x

_drawn_inputs = setup_inputs


def setup_inputs(seed=0):
    import zlib

    import numpy as np

    out = dict(_drawn_inputs(seed))
    spreads = {}
    factors = {'L0_conv_bc': 4.168,
     'L0_conv_Wkk': 64.0,
     'L0_conv_bkk': 8.0,
     'L0_conv_b_ad': 8.0,
     'L0_conv_bf': 4.329}
    for name, (base, spread) in spreads.items():
        noise = np.random.default_rng([zlib.crc32(name.encode()), seed]).standard_normal(out[name].shape)
        drawn = base * np.exp(spread * noise) if base else spread * noise
        out[name] = jnp.asarray(drawn.astype(out[name].dtype))
    for name, factor in factors.items():
        out[name] = (out[name] * factor).astype(out[name].dtype)
    return out
```

```python
from contextlib import ExitStack

import numpy as np

import concourse.bass as bass
import concourse.mybir as mybir
from concourse.alu_op_type import AluOpType as ALU

ACT = mybir.ActivationFunctionType
F32 = mybir.dt.float32
F32R = mybir.dt.float32r
F16 = mybir.dt.float16
I32 = mybir.dt.int32
AX = mybir.AxisListType

P = 128
HALVES = 2
SIDE = 48
PIX = SIDE * SIDE
C = P * HALVES
CM = 64
K = 3
TAPS = K * K
BLOCK = SIDE // K
GROUP = 8
EPS = 1e-5

HROWS = SIDE // 2
HPIX = HROWS * SIDE
CHUNKS = 3
CROWS = HROWS // CHUNKS
CPIX = CROWS * SIDE
LEFT = 2
PITCH = LEFT + SIDE + 2
RING = 4
UNITS = 3
UPIX = PIX // UNITS
SLOTS = 3
MEAN, NEG = TAPS, TAPS + 1
FEATS = TAPS + 2

XN_BOUND = 136.0
F16_SAFE = 30000.0
EXPONENT_BITS = 0x7F800000

BANK = 512
CONV_BANKS = (0, 1)
UNIT_BANKS = (2, 4)
F_BANKS = (2, 3, 6)
STATS_BANK = 7


def wait(eng, sem, images, add=0, per=1):
    value = images * per + add
    if not isinstance(value, int) or value > 0:
        eng.wait_ge(sem, value)


def build(nc, x, wc_nat, wc_t, wf_t, bc, b_ad, bf, wkk, bkk, wck, bck, group_avg, out):
    N = x.shape[0]
    assert N % RING == 0 and N >= 3 * RING
    ctx = ExitStack()
    with ctx:
        def sb(name, shape, dt=F32):
            return ctx.enter_context(nc.sbuf_tensor(name, shape, dt))

        def sem(name):
            return ctx.enter_context(nc.semaphore(name))

        wcn = sb("wcn", [P, C])
        wct = sb("wct", [P, HALVES, P])
        wft = sb("wft", [P, HALVES, P])
        wf_hi = sb("wf_hi", [P, HALVES, P], F32R)
        wf_lo = sb("wf_lo", [P, HALVES, P], F32R)
        bcs = sb("bcs", [P, 1])
        bads = sb("bads", [P, 1])
        bfs = sb("bfs", [P, HALVES])
        out_bias = sb("out_bias", [P, HALVES])
        kk = sb("kk", [P, 2, TAPS])
        ck = sb("ck", [P, 3, CM])
        gavg = sb("gavg", [P, P])
        bnd = sb("bnd", [P, 16])
        X = sb("X", [P, RING, HALVES, PIX])
        RES = sb("RES", [P, 2, HALVES, PIX])
        unused = sb("unused", [P, 2, HALVES, PIX], mybir.dt.bfloat16)
        feats = sb("feats", [P, 2, HALVES, FEATS])
        proj_in = sb("proj_in", [P, 2, HALVES, FEATS])
        neg_mean = sb("neg_mean", [P, 2])
        sq = sb("sq", [P, 2])
        norm = sb("norm", [P, 2, 5])
        wcn_t = sb("wcn_t", [P, 2, HALVES, P])
        pool_g = sb("pool_g", [P, 2, TAPS])
        mean_act = sb("mean_act", [P, 2, TAPS + 1])
        f_bias = sb("f_bias", [P, 2])
        dyn_a = sb("dyn_a", [P, TAPS, CM])
        dyn_b = sb("dyn_b", [P, TAPS, CM])
        dyn_hi = sb("dyn_hi", [P, 2, TAPS, CM], F16)
        dyn_lo = sb("dyn_lo", [P, 2, TAPS, CM], F16)
        f32 = sb("f32", [P, 2, HROWS, SIDE])
        f_lo = sb("f_lo", [P, 2, HROWS, SIDE], F16)
        S = sb("S", [P, 2, SIDE + 2, PITCH], F16)
        Y = sb("Y", [P, 2, 2, HPIX], F32R)
        Yf = Y[:].bitcast(F32)
        ps = ctx.enter_context(nc.psum_tensor("ps", [P, 8, BANK], F32))
        pst = ps[:, STATS_BANK, :]

        const_in = sem("const_in")
        setup_dve = sem("setup_dve")
        pads_zero = sem("pads_zero")
        bound_all = sem("bound_all")
        bias_mm = sem("bias_mm")
        weights_ready = sem("weights_ready")
        loaded = [[sem(f"loaded_{b}_{t}") for t in range(HALVES)] for b in range(RING)]
        stored = [[sem(f"stored_{b}_{t}") for t in range(HALVES)] for b in range(2)]
        means = sem("means")
        maxima = sem("maxima")
        gmean_mm = sem("gmean_mm")
        neg_ready = sem("neg_ready")
        squares = sem("squares")
        gvar_mm = sem("gvar_mm")
        var_ready = sem("var_ready")
        std_ready = sem("std_ready")
        norm_step = sem("norm_step")
        wcn_ready = sem("wcn_ready")
        proj_mm = sem("proj_mm")
        relu_ready = sem("relu_ready")
        fbias_ready = sem("fbias_ready")
        gains_ready = sem("gains_ready")
        dyn_step = sem("dyn_step")
        dyn_ready = sem("dyn_ready")
        f_mm = sem("f_mm")
        f_evac = sem("f_evac")
        flo_ready = sem("flo_ready")
        f_moved = sem("f_moved")
        f_stacked = sem("f_stacked")
        conv_mm = sem("conv_mm")
        y_hi = sem("y_hi")
        y_lo = sem("y_lo")
        out_mm = sem("out_mm")
        result = sem("result")

        xd = x.rearrange("n (p t) f -> n p t f", t=HALVES)
        od = out.rearrange("n (p t) f -> n p t f", t=HALVES)
        DYN_STEPS, NORM_STEPS, OUT_UNITS = 5, 2, HALVES * UNITS
        CONSTS = 15

        def over_images(eng, step):
            for i in range(-2, RING):
                step(i, i % RING)
            with eng.Fori(1, N // RING - 1) as body:
                for u in range(RING):
                    step(body * RING + u, u)
            for i in range(N - RING, N + 1):
                step(i, i % RING)

        def inside(i):
            return not isinstance(i, int) or 0 <= i < N

        def wait_loaded(eng, i, u, t):
            b = (u + 2) % RING
            if isinstance(i, int):
                eng.wait_ge(loaded[b][t], 16 * ((i + 2) // RING + 1))
            else:
                eng.wait_ge(loaded[b][t], i * 4 + (4 * (2 - b) + 16))

        block = ctx.enter_context(nc.Block())

        @block.sync
        def _(sp):
            for lo in (0, CM):
                sp.dma_start(wcn[lo:lo + CM, :], wc_nat).then_inc(const_in, 16)
                sp.dma_start(wct[:, :, lo:lo + CM], wc_t).then_inc(const_in, 16)
                sp.dma_start(wft[lo:lo + CM, :, :], wf_t).then_inc(const_in, 16)
                sp.dma_start(bcs[lo:lo + CM, :], bc).then_inc(const_in, 16)
                sp.dma_start(bads[lo:lo + CM, :], b_ad).then_inc(const_in, 16)
            sp.dma_start(kk[:, 0, :], wkk).then_inc(const_in, 16)
            sp.dma_start(kk[:, 1, :], bkk).then_inc(const_in, 16)
            sp.dma_start(ck[:, 0:2, :], wck).then_inc(const_in, 16)
            sp.dma_start(ck[:, 2, :], bck).then_inc(const_in, 16)
            sp.dma_start(bfs[:], bf).then_inc(const_in, 16)
            for t in range(HALVES):
                sp.dma_start(X[:, 0, t, :], xd[0, :, t, :]).then_inc(loaded[0][t], 16)

            def step(i, u):
                prev, new = i - 1, i + 3
                for t in range(HALVES):
                    if inside(prev):
                        wait(sp, result, prev, UNITS * (t + 1), OUT_UNITS)
                    if inside(new):
                        sp.dma_start(X[:, (u - 1) % RING, t, :], xd[new, :, t, :]) \
                            .then_inc(loaded[(u - 1) % RING][t], 16)
                    if inside(prev):
                        sp.dma_start(od[prev, :, t, :], RES[:, (u - 1) % 2, t, :]) \
                            .then_inc(stored[(u - 1) % 2][t], 16)

            over_images(sp, step)
            for b in range(2):
                for t in range(HALVES):
                    sp.wait_ge(stored[b][t], 16 * (N // 2))

        @block.gpsimd
        def _(pool):
            nc.gpsimd.memset(feats[:], 0.0).then_inc(pads_zero, 1)
            nc.gpsimd.memset(S[:], 0.0).then_inc(pads_zero, 1)
            pool.wait_ge(setup_dve, 3)
            nc.gpsimd.partition_all_reduce(bnd[:, 2:3], bnd[:, 1:2], P, bass.bass_isa.ReduceOp.max) \
                .then_inc(bound_all, 1)
            pool.wait_ge(weights_ready, 1)

            def step(i, u):
                j, par = i + 1, (u + 1) % 2
                if not inside(j):
                    return
                wait(pool, gains_ready, j, 1)
                wait(pool, dyn_ready, j, 0, 2)
                w0 = ck[:, 0:1, :].to_broadcast([P, TAPS, CM])
                w1 = ck[:, 1:2, :].to_broadcast([P, TAPS, CM])
                b0 = ck[:, 2:3, :].to_broadcast([P, TAPS, CM])
                g = pool_g[:, par, :].unsqueeze(2).to_broadcast([P, TAPS, CM])
                s = mean_act[:, par, 0:TAPS].unsqueeze(2).to_broadcast([P, TAPS, CM])
                nc.gpsimd.tensor_tensor(dyn_a[:], w0, g, ALU.mult).then_inc(dyn_step, 1)
                nc.gpsimd.tensor_tensor(dyn_b[:], w1, s, ALU.mult).then_inc(dyn_step, 1)
                wait(pool, dyn_step, j, 2, DYN_STEPS)
                nc.gpsimd.tensor_tensor(dyn_a[:], dyn_a[:], dyn_b[:], ALU.add).then_inc(dyn_step, 1)
                wait(pool, dyn_step, j, 3, DYN_STEPS)
                nc.gpsimd.tensor_tensor(dyn_a[:], dyn_a[:], b0, ALU.add).then_inc(dyn_step, 1)
                wait(pool, dyn_step, j, 4, DYN_STEPS)
                wait(pool, f_evac, j, CHUNKS, CHUNKS)
                nc.gpsimd.tensor_tensor(f_lo[:, par], f32[:, par],
                                        S[:, par, 1:1 + HROWS, LEFT:LEFT + SIDE], ALU.subtract) \
                    .then_inc(flo_ready, 1)
                nc.gpsimd.tensor_scalar(dyn_b[:], dyn_a[:], 0.0, None, ALU.max).then_inc(dyn_step, 1)
                nc.gpsimd.tensor_scalar(dyn_hi[:, par], dyn_a[:], 0.0, None, ALU.max).then_inc(dyn_ready, 1)
                wait(pool, dyn_step, j, 5, DYN_STEPS)
                wait(pool, dyn_ready, j, 1, 2)
                nc.gpsimd.tensor_tensor(dyn_lo[:, par], dyn_b[:], dyn_hi[:, par], ALU.subtract) \
                    .then_inc(dyn_ready, 1)

            over_images(pool, step)

        @block.scalar
        def _(act):
            act.dma_start(gavg[:], group_avg).then_inc(const_in, 16)
            act.wait_ge(pads_zero, 2)

            def step(i, u):
                j, par = i + 1, (u + 1) % 2
                if inside(j):
                    wait(act, fbias_ready, j, 1)
                    for c in range(CHUNKS):
                        rows = slice(CROWS * c, CROWS * (c + 1))
                        src = ps[:, F_BANKS[c], 0:CPIX].rearrange("p (r w) -> p r w", w=SIDE)
                        wait(act, f_mm, j, c + 1, CHUNKS)
                        nc.scalar.activation(S[:, par, 1 + CROWS * c:1 + CROWS * (c + 1), LEFT:LEFT + SIDE],
                                             src, ACT.Relu, bias=f_bias[:, par:par + 1])
                        nc.scalar.activation(f32[:, par, rows, :], src, ACT.Relu,
                                             bias=f_bias[:, par:par + 1]).then_inc(f_evac, 1)
                s, sb_, spar = i + 2, (u + 2) % RING, u % 2
                if inside(s):
                    for t in range(HALVES):
                        wait_loaded(act, i, u, t)
                        nc.scalar.activation(unused[:, 0, t], X[:, sb_, t, :], ACT.Identity,
                                             scale=1.0 / PIX, accum_out=feats[:, spar, t, MEAN:MEAN + 1]) \
                            .then_inc(means, 1)

                def y_high(c):
                    wait(act, conv_mm, i, c + 1, CHUNKS)
                    for h in range(2):
                        lanes = slice(CM * h, CM * (h + 1))
                        nc.scalar.activation(Y[lanes, u % 2, h, CPIX * c:CPIX * (c + 1)],
                                             ps[lanes, CONV_BANKS[(CHUNKS * u + c) % 2], 0:CPIX],
                                             ACT.Copy).then_inc(y_hi, 1)

                if inside(i):
                    y_high(0)
                if inside(s):
                    wait(act, neg_ready, s, 1)
                    nc.scalar.activation(unused[:, 1].rearrange("p t f -> p (t f)"), X[:, sb_].rearrange("p t f -> p (t f)"), ACT.Square,
                                         bias=neg_mean[:, spar:spar + 1],
                                         accum_out=sq[:, spar:spar + 1]).then_inc(squares, 1)
                if inside(i):
                    y_high(1)
                if inside(s):
                    wait(act, var_ready, s, 1)
                    nc.scalar.activation(norm[:, spar, 1:2], norm[:, spar, 0:1], ACT.Sqrt) \
                        .then_inc(std_ready, 1)
                if inside(i):
                    y_high(2)

            over_images(act, step)

        @block.vector
        def _(dve):
            done = [0]

            def link(ins):
                done[0] += 1
                ins.then_inc(setup_dve, 1)
                dve.wait_ge(setup_dve, done[0])

            def pow2_below(col):
                c = bnd[:, col:col + 1].bitcast(I32)
                link(nc.vector.tensor_scalar(c, c, EXPONENT_BITS, None, ALU.bitwise_and))

            dve.wait_ge(const_in, 16 * (CONSTS + 1))
            dve.wait_ge(pads_zero, 2)
            link(nc.vector.tensor_reduce(bnd[:, 0:1], wcn[:], AX.X, ALU.add, apply_absolute_value=True))
            link(nc.vector.tensor_reduce(bnd[:, 15:16], bcs[:], AX.X, ALU.add, apply_absolute_value=True))
            link(nc.vector.scalar_tensor_tensor(out=bnd[:, 1:2], in0=bnd[:, 0:1], scalar=XN_BOUND,
                                                in1=bnd[:, 15:16], op0=ALU.mult, op1=ALU.add))
            dve.wait_ge(bound_all, 1)
            link(nc.vector.tensor_scalar(bnd[:, 3:4], bnd[:, 2:3], 1e-20, 1.0 / F16_SAFE, ALU.max, ALU.mult))
            link(nc.vector.reciprocal(bnd[:, 4:5], bnd[:, 3:4]))
            pow2_below(4)
            link(nc.vector.reciprocal(bnd[:, 5:6], bnd[:, 4:5]))
            link(nc.vector.tensor_reduce(bnd[:, 6:8], kk[:], AX.X, ALU.max, apply_absolute_value=True))
            link(nc.vector.tensor_reduce(bnd[:, 8:11], ck[:], AX.X, ALU.max, apply_absolute_value=True))
            link(nc.vector.scalar_tensor_tensor(out=bnd[:, 11:12], in0=bnd[:, 2:3], scalar=bnd[:, 6:7],
                                                in1=bnd[:, 7:8], op0=ALU.mult, op1=ALU.add))
            link(nc.vector.scalar_tensor_tensor(out=bnd[:, 11:12], in0=bnd[:, 11:12], scalar=bnd[:, 8:9],
                                                in1=bnd[:, 10:11], op0=ALU.mult, op1=ALU.add))
            link(nc.vector.scalar_tensor_tensor(out=bnd[:, 11:12], in0=bnd[:, 2:3], scalar=bnd[:, 9:10],
                                                in1=bnd[:, 11:12], op0=ALU.mult, op1=ALU.add))
            link(nc.vector.tensor_scalar(bnd[:, 11:12], bnd[:, 11:12], 1e-20, 1.0 / F16_SAFE, ALU.max, ALU.mult))
            link(nc.vector.reciprocal(bnd[:, 12:13], bnd[:, 11:12]))
            pow2_below(12)
            link(nc.vector.reciprocal(bnd[:, 13:14], bnd[:, 12:13]))
            dve.wait_ge(bias_mm, 1)
            link(nc.vector.tensor_tensor(out_bias[:], pst[:, 0:HALVES], bfs[:], ALU.add))
            link(nc.vector.tensor_scalar(wft[:], wft[:], bnd[:, 5:6], bnd[:, 13:14], ALU.mult, ALU.mult))
            link(nc.vector.tensor_copy(wf_hi[:], wft[:]))
            link(nc.vector.tensor_tensor(wf_lo[:], wft[:], wf_hi[:].bitcast(F32), ALU.subtract))
            link(nc.vector.tensor_scalar(wct[:], wct[:], bnd[:, 4:5], None, ALU.mult))
            link(nc.vector.tensor_scalar(bcs[:], bcs[:], bnd[:, 4:5], None, ALU.mult))
            link(nc.vector.tensor_scalar(kk[:, 0, :], kk[:, 0, :], bnd[:, 5:6], None, ALU.mult))
            link(nc.vector.tensor_scalar(ck[:], ck[:], bnd[:, 12:13], None, ALU.mult))
            link(nc.vector.tensor_scalar(ck[:, 1, :], ck[:, 1, :], bnd[:, 5:6], None, ALU.mult))
            nc.vector.memset(bnd[:, 14:15], 1.0).then_inc(weights_ready, 1)

            def y_low(i, u, c):
                for h in range(2):
                    src, dst = slice(CM * h, CM * (h + 1)), slice(CM * (1 - h), CM * (2 - h))
                    wait(dve, y_hi, i, 2 * c + h + 1, 2 * CHUNKS)
                    ins = nc.vector.tensor_tensor(Y[dst, u % 2, h, CPIX * c:CPIX * (c + 1)],
                                                  ps[src, CONV_BANKS[(CHUNKS * u + c) % 2], 0:CPIX],
                                                  Yf[src, u % 2, h, CPIX * c:CPIX * (c + 1)], ALU.subtract)
                ins.then_inc(y_lo, 1)

            def unit(j, u, k):
                t, part = divmod(k, UNITS)
                bank = UNIT_BANKS[k % 2]
                span = slice(UPIX * part, UPIX * (part + 1))
                if part == 0 and not (isinstance(j, int) and j < 2):
                    if isinstance(j, int):
                        dve.wait_ge(stored[u % 2][t], 16 * (j // 2))
                    else:
                        dve.wait_ge(stored[u % 2][t], j * 8 - 8 * (u % 2))
                wait(dve, out_mm, j, k + 1, OUT_UNITS)
                nc.vector.scalar_tensor_tensor(
                    out=RES[:, u % 2, t, span].rearrange("p (b f) -> p b f", b=2),
                    in0=ps[:, bank:bank + 2, 0:UPIX // 2], scalar=out_bias[:, t:t + 1],
                    in1=X[:, u, t, span].rearrange("p (b f) -> p b f", b=2),
                    op0=ALU.add, op1=ALU.add).then_inc(result, 1)

            def step(i, u):
                j, par, s, spar, sb_ = i + 1, (u + 1) % 2, i + 2, u % 2, (u + 2) % RING
                prev, pu = i - 1, (u - 1) % RING
                if inside(prev):
                    y_low(prev, pu, 2)
                if inside(s):
                    for t in range(HALVES):
                        wait_loaded(dve, i, u, t)
                        blocks = X[:, sb_, t, :].rearrange("p (k h l w) -> p k l h w", k=K, h=BLOCK, l=K)
                        nc.vector.tensor_reduce(
                            feats[:, spar, t, 0:TAPS].rearrange("p (k l) -> p k l", k=K),
                            blocks, AX.XY, ALU.max).then_inc(maxima, 1)
                if inside(prev):
                    unit(prev, pu, 0)
                if inside(j):
                    top, bottom = slice(1, 1 + HROWS), slice(1 + HROWS, 1 + SIDE)
                    cols = slice(LEFT, LEFT + SIDE)
                    wait(dve, flo_ready, j, 1)
                    nc.vector.tensor_copy(S[0:CM, par, bottom, cols], S[CM:P, par, top, cols]) \
                        .then_inc(f_moved, 1)
                    nc.vector.tensor_copy(S[CM:P, par, bottom, cols], f_lo[CM:P, par])
                    wait(dve, f_moved, j, 1)
                    nc.vector.tensor_copy(S[CM:P, par, top, cols], f_lo[0:CM, par]).then_inc(f_stacked, 1)
                if inside(s):
                    wait(dve, gmean_mm, s, 1)
                    nc.vector.tensor_scalar(neg_mean[:, spar:spar + 1], pst[:, 0:1], -1.0, None, ALU.mult) \
                        .then_inc(neg_ready, 1)
                if inside(prev):
                    unit(prev, pu, 1)
                if inside(i):
                    y_low(i, u, 0)
                if inside(prev):
                    unit(prev, pu, 2)
                if inside(prev):
                    unit(prev, pu, 3)
                if inside(i):
                    y_low(i, u, 1)
                if inside(prev):
                    unit(prev, pu, 4)
                    unit(prev, pu, 5)
                if inside(s):
                    var, std, r0, e, half = (norm[:, spar, q:q + 1] for q in range(5))
                    wait(dve, gvar_mm, s, 1)
                    nc.vector.tensor_scalar(var, pst[:, 1:2], 1.0 / PIX, EPS, ALU.mult, ALU.add) \
                        .then_inc(var_ready, 1)
                    wait(dve, neg_ready, s, 1)
                    wait(dve, maxima, s, HALVES, HALVES)
                    wait(dve, means, s, HALVES, HALVES)
                    nc.vector.tensor_scalar(proj_in[:, spar], feats[:, spar], neg_mean[:, spar:spar + 1],
                                            None, ALU.add)
                    wait(dve, std_ready, s, 1)
                    nc.vector.reciprocal(r0, std).then_inc(norm_step, 1)
                    wait(dve, norm_step, s, 1, NORM_STEPS + 1)
                    nc.vector.scalar_tensor_tensor(out=e, in0=r0, scalar=var, in1=r0,
                                                   op0=ALU.mult, op1=ALU.mult).then_inc(norm_step, 1)
                    wait(dve, norm_step, s, 2, NORM_STEPS + 1)
                    nc.vector.tensor_scalar(half, e, -0.5, 1.5, ALU.mult, ALU.add).then_inc(norm_step, 1)
                    wait(dve, norm_step, s, 3, NORM_STEPS + 1)
                    nc.vector.tensor_scalar(wcn_t[:, spar], wct[:], r0, half, ALU.mult, ALU.mult) \
                        .then_inc(wcn_ready, 1)
                if inside(s):
                    wait(dve, proj_mm, s, 1)
                    nc.vector.tensor_scalar(mean_act[:, spar], pst[:, 4:4 + TAPS + 1], bcs[:], 0.0,
                                            ALU.add, ALU.max).then_inc(relu_ready, 1)
                    nc.vector.tensor_scalar(f_bias[:, spar:spar + 1], pst[:, 4 + NEG:5 + NEG], bcs[:], None,
                                            ALU.add).then_inc(fbias_ready, 1)
                    wait(dve, relu_ready, s, 1)
                    nc.vector.scalar_tensor_tensor(out=pool_g[:, spar, :], in0=kk[:, 0, :],
                                                   scalar=mean_act[:, spar, MEAN:MEAN + 1],
                                                   in1=kk[:, 1, :], op0=ALU.mult, op1=ALU.add) \
                        .then_inc(gains_ready, 1)

            over_images(dve, step)

        @block.tensor
        def _(pe):
            pe.wait_ge(const_in, 16 * (CONSTS + 1))
            for t in range(HALVES):
                mm = nc.tensor.matmul(pst[:, t:t + 1], wft[0:CM, t, :], bads[0:CM, :], start=True, stop=True)
            mm.then_inc(bias_mm, 1)
            pe.wait_ge(weights_ready, 1)

            def step(i, u):
                j, s, spar = i + 1, i + 2, u % 2
                prev, pu = i - 1, (u - 1) % RING
                if inside(j):
                    wait(pe, wcn_ready, j, 1)
                    for c in range(CHUNKS):
                        if c < 2:
                            if inside(i - 2):
                                wait(pe, result, i - 2, 5, OUT_UNITS)
                        else:
                            wait(pe, f_evac, i, CHUNKS, CHUNKS)
                        for t in range(HALVES):
                            for h in range(2):
                                at = HPIX * h + CPIX * c
                                mm = nc.tensor.matmul(ps[CM * h:CM * (h + 1), F_BANKS[c], 0:CPIX],
                                                      wcn_t[:, (u + 1) % 2, t, 0:CM],
                                                      X[:, (u + 1) % RING, t, at:at + CPIX],
                                                      start=(t == 0), stop=(t == HALVES - 1))
                        mm.then_inc(f_mm, 1)

                def unit(k):
                    if not inside(prev):
                        return
                    t, part = divmod(k, UNITS)
                    if k == 0:
                        wait(pe, y_lo, prev, CHUNKS, CHUNKS)
                        if inside(j):
                            wait(pe, f_evac, j, 2, CHUNKS)
                    wait(pe, result, prev, k - 1, OUT_UNITS)
                    for q in range(2):
                        at = UPIX * part + CPIX * q
                        src = Y[:, pu % 2, at // HPIX, at % HPIX:at % HPIX + CPIX]
                        for w in (wf_hi, wf_lo):
                            mm = nc.tensor.matmul(ps[:, UNIT_BANKS[k % 2] + q, 0:CPIX], w[:, t, :], src,
                                                  start=(w is wf_hi), stop=(w is wf_lo))
                    mm.then_inc(out_mm, 1)

                def conv(slot):
                    if not inside(i):
                        return
                    c, part = divmod(slot, SLOTS)
                    if part == 0:
                        if c == 0:
                            wait(pe, f_stacked, i, 1)
                            wait(pe, dyn_ready, i, 2, 2)
                        wait(pe, y_lo, i, c - 1, CHUNKS)
                    passes = [(w, tap) for w in (dyn_hi, dyn_lo) for tap in range(TAPS)]
                    some = len(passes) // SLOTS
                    for n in range(some * part, some * (part + 1)):
                        w, tap = passes[n]
                        dy, dx = divmod(tap, K)
                        for h in range(2):
                            r = HROWS * h + CROWS * c + dy
                            mm = nc.tensor.matmul(
                                ps[CM * h:CM * (h + 1), CONV_BANKS[(CHUNKS * u + c) % 2], 0:CPIX],
                                w[:, u % 2, tap, :],
                                S[:, u % 2, r:r + CROWS, LEFT - 1 + dx:LEFT - 1 + dx + SIDE],
                                start=(n == 0), stop=(n == len(passes) - 1))
                    if part == SLOTS - 1:
                        mm.then_inc(conv_mm, 1)

                def group_mean():
                    if inside(s):
                        wait(pe, means, s, HALVES, HALVES)
                        wait(pe, gains_ready, j, 1)
                        for t in range(HALVES):
                            mm = nc.tensor.matmul(pst[:, 0:1], gavg[:], feats[:, spar, t, MEAN:MEAN + 1],
                                                  start=(t == 0), stop=(t == HALVES - 1))
                        mm.then_inc(gmean_mm, 1)

                def group_var():
                    if inside(s):
                        wait(pe, squares, s, 1)
                        nc.tensor.matmul(pst[:, 1:2], gavg[:], sq[:, spar:spar + 1], start=True, stop=True) \
                            .then_inc(gvar_mm, 1)

                def project():
                    if inside(s):
                        wait(pe, wcn_ready, s, 1)
                        for t in range(HALVES):
                            mm = nc.tensor.matmul(pst[:, 4:4 + FEATS], wcn_t[:, spar, t, :],
                                                  proj_in[:, spar, t, :],
                                                  start=(t == 0), stop=(t == HALVES - 1))
                        mm.then_inc(proj_mm, 1)

                conv(0)
                conv(1)
                unit(0)
                conv(2)
                unit(1)
                group_mean()
                conv(3)
                unit(2)
                conv(4)
                unit(3)
                conv(5)
                unit(4)
                conv(6)
                unit(5)
                group_var()
                conv(7)
                conv(8)
                project()

            over_images(pe, step)


def kernel(x, L0_conv_Wc, L0_conv_bc, L0_conv_Wkk, L0_conv_bkk, L0_conv_Wck, L0_conv_bck,
           L0_conv_b_ad, L0_conv_Wf, L0_conv_bf):
    import concourse.bacc as bacc
    from concourse.bass_utils import run_bass_kernel_spmd

    x = np.asarray(x)
    n = x.shape[0]
    rows = lambda a, *shape: np.ascontiguousarray(np.broadcast_to(np.asarray(a), (P, *shape)))
    arrays = {
        "x": x.reshape(n, C, PIX),
        "wc_nat": np.asarray(L0_conv_Wc),
        "wc_t": np.ascontiguousarray(np.asarray(L0_conv_Wc).T).reshape(P, HALVES, CM),
        "wf_t": np.ascontiguousarray(np.asarray(L0_conv_Wf).reshape(P, HALVES, CM).transpose(2, 1, 0)),
        "bc": np.asarray(L0_conv_bc).reshape(CM, 1),
        "b_ad": np.asarray(L0_conv_b_ad).reshape(CM, 1),
        "bf": np.asarray(L0_conv_bf).reshape(P, HALVES),
        "wkk": rows(L0_conv_Wkk, TAPS),
        "bkk": rows(L0_conv_bkk, TAPS),
        "wck": rows(np.asarray(L0_conv_Wck).T, 2, CM),
        "bck": rows(L0_conv_bck, CM),
        "group_avg": np.kron(np.eye(P * HALVES // GROUP), np.full((GROUP // HALVES,) * 2, 1.0 / GROUP))
        .astype(np.float32),
    }
    nc = bacc.Bacc("TRN2", target_bir_lowering=False, num_devices=1)
    args = [nc.dram_tensor(k, a.shape, mybir.dt.from_np(a.dtype), kind="ExternalInput").ap()
            for k, a in arrays.items()]
    out = nc.dram_tensor("out", (n, C, PIX), F32, kind="ExternalOutput").ap()
    build(nc, *args, out)
    r = run_bass_kernel_spmd(nc, [arrays], core_ids=[0])
    return r.results[0]["out"].reshape(x.shape)
```

```python
from contextlib import ExitStack

import numpy as np

import concourse.bass as bass
import concourse.mybir as mybir
from concourse.alu_op_type import AluOpType as ALU

ACT = mybir.ActivationFunctionType
F32 = mybir.dt.float32
F32R = mybir.dt.float32r
F16 = mybir.dt.float16
I32 = mybir.dt.int32
AX = mybir.AxisListType

P = 128
HALVES = 2
SIDE = 48
PIX = SIDE * SIDE
C = P * HALVES
CM = 64
K = 3
TAPS = K * K
BLOCK = SIDE // K
GROUP = 8
EPS = 1e-5

HROWS = SIDE // 2
HPIX = HROWS * SIDE
CHUNKS = 3
CROWS = HROWS // CHUNKS
CPIX = CROWS * SIDE
LEFT = 2
PITCH = LEFT + SIDE + 2
RING = 4
UNITS = 3
UPIX = PIX // UNITS
SLOTS = 5
MEAN, NEG = TAPS, TAPS + 1
FEATS = TAPS + 2

XN_BOUND = 136.0
F16_SAFE = 30000.0
EXPONENT_BITS = 0x7F800000

BANK = 512
CONV_BANKS = (0, 1)
UNIT_BANKS = (2, 4)
F_BANKS = (6, 2, 3)
STATS_BANK = 7


def wait(eng, sem, images, add=0, per=1):
    value = images * per + add
    if not isinstance(value, int) or value > 0:
        eng.wait_ge(sem, value)


CONST_COLS = {
    "wc_nat": C,
    "wc_t": HALVES * P,
    "wf_t": HALVES * P,
    "bc": 1,
    "b_ad": 1,
    "bf": HALVES,
    "kk": 2 * TAPS,
    "ck": 3 * CM,
    "group_avg": P,
}


def build(nc, x, consts, out):
    N = x.shape[0]
    assert N % RING == 0 and N >= 3 * RING
    ctx = ExitStack()
    with ctx:
        def sb(name, shape, dt=F32):
            return ctx.enter_context(nc.sbuf_tensor(name, shape, dt))

        def sem(name):
            return ctx.enter_context(nc.semaphore(name))

        const = sb("const", [P, sum(CONST_COLS.values())])
        first = dict(zip(CONST_COLS, np.cumsum([0, *CONST_COLS.values()]).tolist()))

        def part(name):
            return const[:, first[name]:first[name] + CONST_COLS[name]]

        wcn, bcs, bads, bfs, gavg = (part(name) for name in ("wc_nat", "bc", "b_ad", "bf", "group_avg"))
        wct = part("wc_t").rearrange("p (t o) -> p t o", t=HALVES)
        wft = part("wf_t").rearrange("p (t o) -> p t o", t=HALVES)
        kk = part("kk").rearrange("p (k l) -> p k l", k=2)
        ck = part("ck").rearrange("p (k o) -> p k o", k=3)
        wf_hi = sb("wf_hi", [P, HALVES, P], F32R)
        wf_lo = sb("wf_lo", [P, HALVES, P], F32R)
        out_bias = sb("out_bias", [P, HALVES])
        bnd = sb("bnd", [P, 16])
        X = sb("X", [P, RING, HALVES, PIX])
        RES = sb("RES", [P, 2, HALVES, PIX])
        unused = sb("unused", [P, 2, HALVES, PIX], mybir.dt.bfloat16)
        feats = sb("feats", [P, 2, HALVES, FEATS])
        proj_in = sb("proj_in", [P, 2, HALVES, FEATS])
        neg_mean = sb("neg_mean", [P, 2])
        sq = sb("sq", [P, 2, HALVES])
        norm = sb("norm", [P, 2, 5])
        wcn_t = sb("wcn_t", [P, 2, HALVES, P])
        pool_g = sb("pool_g", [P, 2, TAPS])
        mean_act = sb("mean_act", [P, 2, TAPS + 1])
        f_bias = sb("f_bias", [P, 2])
        dyn_a = sb("dyn_a", [P, TAPS, CM])
        dyn_b = sb("dyn_b", [P, TAPS, CM])
        dyn_hi = sb("dyn_hi", [P, 2, TAPS, CM], F16)
        dyn_lo = sb("dyn_lo", [P, 2, TAPS, CM], F16)
        f32 = sb("f32", [P, 2, HROWS, SIDE])
        f_lo = sb("f_lo", [P, 2, HROWS, SIDE], F16)
        S = sb("S", [P, 2, SIDE + 2, PITCH], F16)
        Q = sb("Q", [P, 2, SIDE, PITCH], F16)
        Y = sb("Y", [P, 2, 2, HPIX], F32R)
        Yf = Y[:].bitcast(F32)
        ps = ctx.enter_context(nc.psum_tensor("ps", [P, 8, BANK], F32))
        pst = ps[:, STATS_BANK, :]

        const_in = sem("const_in")
        setup_dve = sem("setup_dve")
        pads_zero = sem("pads_zero")
        bound_all = sem("bound_all")
        bias_mm = sem("bias_mm")
        weights_ready = sem("weights_ready")
        loaded = [[sem(f"loaded_{b}_{t}") for t in range(HALVES)] for b in range(RING)]
        stored = [[sem(f"stored_{b}_{t}") for t in range(HALVES)] for b in range(2)]
        means = sem("means")
        maxima = sem("maxima")
        gmean_mm = sem("gmean_mm")
        neg_ready = sem("neg_ready")
        squares = sem("squares")
        gvar_mm = sem("gvar_mm")
        var_ready = sem("var_ready")
        std_ready = sem("std_ready")
        norm_step = sem("norm_step")
        wcn_ready = sem("wcn_ready")
        proj_mm = sem("proj_mm")
        relu_ready = sem("relu_ready")
        fbias_ready = sem("fbias_ready")
        gains_ready = sem("gains_ready")
        dyn_step = sem("dyn_step")
        dyn_ready = sem("dyn_ready")
        dyn_paired = sem("dyn_paired")
        f_mm = sem("f_mm")
        f_evac = sem("f_evac")
        flo_ready = sem("flo_ready")
        f_moved = sem("f_moved")
        f_stacked = sem("f_stacked")
        q_upper = sem("q_upper")
        conv_mm = sem("conv_mm")
        y_hi = sem("y_hi")
        y_lo = sem("y_lo")
        out_mm = sem("out_mm")
        result = sem("result")

        xd = x.rearrange("n (p t) f -> n p t f", t=HALVES)
        od = out.rearrange("n (p t) f -> n p t f", t=HALVES)
        DYN_STEPS, NORM_STEPS, OUT_UNITS = 5, 3, HALVES * UNITS

        def over_images(eng, step):
            for i in range(-2, RING):
                step(i, i % RING)
            with eng.Fori(1, N // RING - 1) as body:
                for u in range(RING):
                    step(body * RING + u, u)
            for i in range(N - RING, N + 1):
                step(i, i % RING)

        def inside(i):
            return not isinstance(i, int) or 0 <= i < N

        def wait_loaded(eng, i, u, t):
            b = (u + 2) % RING
            if isinstance(i, int):
                eng.wait_ge(loaded[b][t], 16 * ((i + 2) // RING + 1))
            else:
                eng.wait_ge(loaded[b][t], i * 4 + (4 * (2 - b) + 16))

        block = ctx.enter_context(nc.Block())

        @block.sync
        def _(sp):
            sp.dma_start(X[:, 0, 0, :], xd[0, :, 0, :]).then_inc(loaded[0][0], 16)
            sp.dma_start(const[:], consts).then_inc(const_in, 16)
            sp.dma_start(X[:, 0, 1, :], xd[0, :, 1, :]).then_inc(loaded[0][1], 16)

            def store(prev, u, t):
                sp.dma_start(od[prev, :, t, :], RES[:, (u - 1) % 2, t, :]).then_inc(stored[(u - 1) % 2][t], 16)

            def step(i, u):
                prev, new = i - 1, i + 3
                for t in range(HALVES):
                    if inside(prev):
                        wait(sp, result, prev, UNITS * (t + 1), OUT_UNITS)
                    if inside(new):
                        sp.dma_start(X[:, (u - 1) % RING, t, :], xd[new, :, t, :]) \
                            .then_inc(loaded[(u - 1) % RING][t], 16)
                    elif inside(prev):
                        store(prev, u, t)
                if inside(prev) and inside(new):
                    for t in range(HALVES):
                        store(prev, u, t)

            over_images(sp, step)
            for b in range(2):
                for t in range(HALVES):
                    sp.wait_ge(stored[b][t], 16 * (N // 2))

        @block.gpsimd
        def _(pool):
            nc.gpsimd.memset(feats[:], 0.0).then_inc(pads_zero, 1)
            nc.gpsimd.memset(S[:], 0.0).then_inc(pads_zero, 1)
            nc.gpsimd.memset(Q[:], 0.0).then_inc(pads_zero, 1)
            pool.wait_ge(setup_dve, 3)
            nc.gpsimd.partition_all_reduce(bnd[:, 2:3], bnd[:, 1:2], P, bass.bass_isa.ReduceOp.max) \
                .then_inc(bound_all, 1)
            pool.wait_ge(weights_ready, 1)

            def step(i, u):
                j, par = i + 1, (u + 1) % 2
                if not inside(j):
                    return
                wait(pool, gains_ready, j, 1)
                wait(pool, dyn_ready, j, 0, 2)
                w0 = ck[:, 0:1, :].to_broadcast([P, TAPS, CM])
                w1 = ck[:, 1:2, :].to_broadcast([P, TAPS, CM])
                b0 = ck[:, 2:3, :].to_broadcast([P, TAPS, CM])
                g = pool_g[:, par, :].unsqueeze(2).to_broadcast([P, TAPS, CM])
                s = mean_act[:, par, 0:TAPS].unsqueeze(2).to_broadcast([P, TAPS, CM])
                nc.gpsimd.tensor_tensor(dyn_a[:], w0, g, ALU.mult).then_inc(dyn_step, 1)
                nc.gpsimd.tensor_tensor(dyn_b[:], w1, s, ALU.mult).then_inc(dyn_step, 1)
                wait(pool, dyn_step, j, 2, DYN_STEPS)
                nc.gpsimd.tensor_tensor(dyn_a[:], dyn_a[:], dyn_b[:], ALU.add).then_inc(dyn_step, 1)
                wait(pool, dyn_step, j, 3, DYN_STEPS)
                nc.gpsimd.tensor_tensor(dyn_a[:], dyn_a[:], b0, ALU.add).then_inc(dyn_step, 1)
                wait(pool, dyn_step, j, 4, DYN_STEPS)
                wait(pool, f_evac, j, CHUNKS, CHUNKS)
                nc.gpsimd.tensor_tensor(f_lo[:, par], f32[:, par],
                                        S[:, par, 1:1 + HROWS, LEFT:LEFT + SIDE], ALU.subtract) \
                    .then_inc(flo_ready, 1)
                nc.gpsimd.tensor_scalar(dyn_b[:], dyn_a[:], 0.0, None, ALU.max).then_inc(dyn_step, 1)
                nc.gpsimd.tensor_scalar(dyn_hi[:, par], dyn_a[:], 0.0, None, ALU.max).then_inc(dyn_ready, 1)
                wait(pool, dyn_step, j, 5, DYN_STEPS)
                wait(pool, dyn_ready, j, 1, 2)
                nc.gpsimd.tensor_tensor(dyn_lo[:, par], dyn_b[:], dyn_hi[:, par], ALU.subtract) \
                    .then_inc(dyn_ready, 1)

            over_images(pool, step)

        @block.scalar
        def _(act):
            act.wait_ge(pads_zero, 1)

            def step(i, u):
                j, par = i + 1, (u + 1) % 2
                s, slot, spar = i + 2, (u + 2) % RING, u % 2

                def f_out(c):
                    if not inside(j):
                        return
                    src = ps[:, F_BANKS[c], 0:CPIX].rearrange("p (r w) -> p r w", w=SIDE)
                    if c == 0:
                        wait(act, fbias_ready, j, 1)
                        if isinstance(i, int) and i == -1:
                            act.wait_ge(pads_zero, 3)
                    wait(act, f_mm, j, c + 1, CHUNKS)
                    nc.scalar.activation(S[:, par, 1 + CROWS * c:1 + CROWS * (c + 1), LEFT:LEFT + SIDE],
                                         src, ACT.Relu, bias=f_bias[:, par:par + 1])
                    nc.scalar.activation(f32[:, par, CROWS * c:CROWS * (c + 1), :], src, ACT.Relu,
                                         bias=f_bias[:, par:par + 1]).then_inc(f_evac, 1)

                def channel_means(t):
                    if inside(s):
                        wait_loaded(act, i, u, t)
                        nc.scalar.activation(unused[:, 0, t], X[:, slot, t, :], ACT.Identity,
                                             scale=1.0 / PIX, accum_out=feats[:, spar, t, MEAN:MEAN + 1]) \
                            .then_inc(means, 1)

                def square_sum(t):
                    if inside(s):
                        if t == 0:
                            wait(act, neg_ready, s, 1)
                        nc.scalar.activation(unused[:, 1, t], X[:, slot, t, :], ACT.Square,
                                             bias=neg_mean[:, spar:spar + 1],
                                             accum_out=sq[:, spar, t:t + 1]).then_inc(squares, 1)

                def deviation():
                    if inside(s):
                        wait(act, var_ready, s, 1)
                        nc.scalar.activation(norm[:, spar, 1:2], norm[:, spar, 0:1], ACT.Sqrt) \
                            .then_inc(std_ready, 1)

                def q_up(h):
                    if inside(j):
                        if h == 0:
                            wait(act, f_evac, j, CHUNKS, CHUNKS)
                        else:
                            wait(act, f_moved, j, 1)
                        rows = slice(HROWS * h, HROWS * (h + 1))
                        nc.scalar.activation(Q[CM:P, par, rows, LEFT:LEFT + SIDE],
                                             S[0:CM, par, 1 + HROWS * h:1 + HROWS * (h + 1), LEFT:LEFT + SIDE],
                                             ACT.Copy).then_inc(q_upper, 1)

                def y_high(c):
                    if not inside(i):
                        return
                    wait(act, conv_mm, i, c + 1, CHUNKS)
                    for h in range(2):
                        lanes = slice(CM * h, CM * (h + 1))
                        nc.scalar.activation(Y[lanes, u % 2, h, CPIX * c:CPIX * (c + 1)],
                                             ps[lanes, CONV_BANKS[(CHUNKS * u + c) % 2], 0:CPIX],
                                             ACT.Copy).then_inc(y_hi, 1)

                if isinstance(i, int) and i == -1:
                    channel_means(0)
                    channel_means(1)
                    f_out(0)
                    f_out(1)
                    f_out(2)
                    square_sum(0)
                    square_sum(1)
                    q_up(0)
                    q_up(1)
                    deviation()
                else:
                    f_out(0)
                    channel_means(0)
                    f_out(1)
                    f_out(2)
                    channel_means(1)
                    y_high(0)
                    square_sum(0)
                    square_sum(1)
                    y_high(1)
                    deviation()
                    q_up(1)
                    q_up(0)
                    y_high(2)

            over_images(act, step)

        @block.vector
        def _(dve):
            done = [0]

            def link(ins):
                done[0] += 1
                ins.then_inc(setup_dve, 1)
                dve.wait_ge(setup_dve, done[0])

            def pow2_below(col):
                c = bnd[:, col:col + 1].bitcast(I32)
                link(nc.vector.tensor_scalar(c, c, EXPONENT_BITS, None, ALU.bitwise_and))

            dve.wait_ge(const_in, 16)
            dve.wait_ge(pads_zero, 1)
            link(nc.vector.tensor_reduce(bnd[:, 0:1], wcn[:], AX.X, ALU.add, apply_absolute_value=True))
            link(nc.vector.tensor_reduce(bnd[:, 15:16], bcs[:], AX.X, ALU.add, apply_absolute_value=True))
            link(nc.vector.scalar_tensor_tensor(out=bnd[:, 1:2], in0=bnd[:, 0:1], scalar=XN_BOUND,
                                                in1=bnd[:, 15:16], op0=ALU.mult, op1=ALU.add))
            dve.wait_ge(bound_all, 1)
            link(nc.vector.tensor_scalar(bnd[:, 3:4], bnd[:, 2:3], 1e-20, 1.0 / F16_SAFE, ALU.max, ALU.mult))
            link(nc.vector.reciprocal(bnd[:, 4:5], bnd[:, 3:4]))
            pow2_below(4)
            link(nc.vector.reciprocal(bnd[:, 5:6], bnd[:, 4:5]))
            link(nc.vector.tensor_reduce(bnd[:, 6:8], kk[:], AX.X, ALU.max, apply_absolute_value=True))
            link(nc.vector.tensor_reduce(bnd[:, 8:11], ck[:], AX.X, ALU.max, apply_absolute_value=True))
            link(nc.vector.scalar_tensor_tensor(out=bnd[:, 11:12], in0=bnd[:, 2:3], scalar=bnd[:, 6:7],
                                                in1=bnd[:, 7:8], op0=ALU.mult, op1=ALU.add))
            link(nc.vector.scalar_tensor_tensor(out=bnd[:, 11:12], in0=bnd[:, 11:12], scalar=bnd[:, 8:9],
                                                in1=bnd[:, 10:11], op0=ALU.mult, op1=ALU.add))
            link(nc.vector.scalar_tensor_tensor(out=bnd[:, 11:12], in0=bnd[:, 2:3], scalar=bnd[:, 9:10],
                                                in1=bnd[:, 11:12], op0=ALU.mult, op1=ALU.add))
            link(nc.vector.tensor_scalar(bnd[:, 11:12], bnd[:, 11:12], 1e-20, 1.0 / F16_SAFE, ALU.max, ALU.mult))
            link(nc.vector.reciprocal(bnd[:, 12:13], bnd[:, 11:12]))
            pow2_below(12)
            link(nc.vector.reciprocal(bnd[:, 13:14], bnd[:, 12:13]))
            dve.wait_ge(bias_mm, 1)
            link(nc.vector.tensor_tensor(out_bias[:], pst[:, 0:HALVES], bfs[:], ALU.add))
            link(nc.vector.tensor_scalar(wft[:], wft[:], bnd[:, 5:6], bnd[:, 13:14], ALU.mult, ALU.mult))
            link(nc.vector.tensor_copy(wf_hi[:], wft[:]))
            link(nc.vector.tensor_tensor(wf_lo[:], wft[:], wf_hi[:].bitcast(F32), ALU.subtract))
            link(nc.vector.tensor_scalar(wct[:], wct[:], bnd[:, 4:5], None, ALU.mult))
            link(nc.vector.tensor_scalar(bcs[:], bcs[:], bnd[:, 4:5], None, ALU.mult))
            link(nc.vector.tensor_scalar(kk[:, 0, :], kk[:, 0, :], bnd[:, 5:6], None, ALU.mult))
            link(nc.vector.tensor_scalar(ck[:], ck[:], bnd[:, 12:13], None, ALU.mult))
            link(nc.vector.tensor_scalar(ck[:, 1, :], ck[:, 1, :], bnd[:, 5:6], None, ALU.mult))
            nc.vector.memset(bnd[:, 14:15], 1.0).then_inc(weights_ready, 1)

            def step(i, u):
                j, par, s, spar = i + 1, (u + 1) % 2, i + 2, u % 2
                prev, pu = i - 1, (u - 1) % RING
                top, bottom = slice(1, 1 + HROWS), slice(1 + HROWS, 1 + SIDE)
                cols = slice(LEFT, LEFT + SIDE)
                var, std, r0, e, half = (norm[:, spar, q:q + 1] for q in range(5))

                def y_low(c, i=i, u=u):
                    if not inside(i):
                        return
                    for h in range(2):
                        src, dst = slice(CM * h, CM * (h + 1)), slice(CM * (1 - h), CM * (2 - h))
                        wait(dve, y_hi, i, 2 * c + h + 1, 2 * CHUNKS)
                        ins = nc.vector.tensor_tensor(Y[dst, u % 2, h, CPIX * c:CPIX * (c + 1)],
                                                      ps[src, CONV_BANKS[(CHUNKS * u + c) % 2], 0:CPIX],
                                                      Yf[src, u % 2, h, CPIX * c:CPIX * (c + 1)], ALU.subtract)
                    ins.then_inc(y_lo, 1)

                def pair_taps():
                    if inside(i):
                        wait(dve, dyn_ready, i, 2, 2)
                        nc.vector.tensor_copy(dyn_lo[CM:P, u % 2, 0:K], dyn_lo[CM:P, u % 2, K:2 * K]) \
                            .then_inc(dyn_paired, 1)

                def maximum(t, k):
                    if inside(s):
                        wait_loaded(dve, i, u, t)
                        rows = slice(BLOCK * SIDE * k, BLOCK * SIDE * (k + 1))
                        nc.vector.tensor_reduce(
                            feats[:, spar, t, K * k:K * (k + 1)],
                            X[:, (u + 2) % RING, t, rows].rearrange("p (h l w) -> p l h w", h=BLOCK, l=K),
                            AX.XY, ALU.max).then_inc(maxima, 1)

                def move_b():
                    if inside(j):
                        wait(dve, f_evac, j, CHUNKS, CHUNKS)
                        nc.vector.tensor_copy(S[0:CM, par, bottom, cols], S[CM:P, par, top, cols]) \
                            .then_inc(f_moved, 1)

                def q_low(h):
                    if inside(j):
                        if isinstance(i, int) and i == -1:
                            dve.wait_ge(pads_zero, 3)
                        if h == 0:
                            wait(dve, f_evac, j, CHUNKS, CHUNKS)
                        else:
                            wait(dve, f_moved, j, 1)
                        rows = slice(1, 1 + HROWS) if h == 0 else slice(1 + HROWS, SIDE)
                        nc.vector.tensor_copy(Q[0:CM, par, rows, :], S[0:CM, par, rows, :])

                def stack_low(rows, lanes):
                    if inside(j):
                        wait(dve, flo_ready, j, 1)
                        nc.vector.tensor_copy(S[CM:P, par, rows, cols], f_lo[lanes, par]).then_inc(f_stacked, 1)

                def negate_mean():
                    if inside(s):
                        wait(dve, gmean_mm, s, 1)
                        nc.vector.tensor_scalar(neg_mean[:, spar:spar + 1], pst[:, 0:1], -1.0, None, ALU.mult) \
                            .then_inc(neg_ready, 1)

                def variance():
                    if inside(s):
                        wait(dve, gvar_mm, s, 1)
                        nc.vector.tensor_scalar(var, pst[:, 1:2], 1.0 / PIX, EPS, ALU.mult, ALU.add) \
                            .then_inc(var_ready, 1)
                        wait(dve, neg_ready, s, 1)
                        wait(dve, maxima, s, HALVES * K, HALVES * K)
                        wait(dve, means, s, HALVES, HALVES)
                        nc.vector.tensor_scalar(proj_in[:, spar], feats[:, spar], neg_mean[:, spar:spar + 1],
                                                None, ALU.add)

                def normalise():
                    if inside(s):
                        wait(dve, std_ready, s, 1)
                        nc.vector.reciprocal(r0, std).then_inc(norm_step, 1)
                        wait(dve, norm_step, s, 1, NORM_STEPS)
                        nc.vector.scalar_tensor_tensor(out=e, in0=r0, scalar=var, in1=r0,
                                                       op0=ALU.mult, op1=ALU.mult).then_inc(norm_step, 1)
                        wait(dve, norm_step, s, 2, NORM_STEPS)
                        nc.vector.tensor_scalar(half, e, -0.5, 1.5, ALU.mult, ALU.add).then_inc(norm_step, 1)
                        wait(dve, norm_step, s, 3, NORM_STEPS)
                        nc.vector.tensor_scalar(wcn_t[:, spar], wct[:], r0, half, ALU.mult, ALU.mult) \
                            .then_inc(wcn_ready, 1)

                def gains():
                    if inside(s):
                        wait(dve, proj_mm, s, 1)
                        nc.vector.tensor_scalar(f_bias[:, spar:spar + 1], pst[:, 4 + NEG:5 + NEG], bcs[:], None,
                                                ALU.add).then_inc(fbias_ready, 1)
                        nc.vector.tensor_scalar(mean_act[:, spar], pst[:, 4:4 + TAPS + 1], bcs[:], 0.0,
                                                ALU.add, ALU.max).then_inc(relu_ready, 1)
                        wait(dve, relu_ready, s, 1)
                        nc.vector.scalar_tensor_tensor(out=pool_g[:, spar, :], in0=kk[:, 0, :],
                                                       scalar=mean_act[:, spar, MEAN:MEAN + 1],
                                                       in1=kk[:, 1, :], op0=ALU.mult, op1=ALU.add) \
                            .then_inc(gains_ready, 1)

                def unit(k):
                    if not inside(prev):
                        return
                    t, part = divmod(k, UNITS)
                    bank = UNIT_BANKS[k % 2]
                    span = slice(UPIX * part, UPIX * (part + 1))
                    if part == 0 and not (isinstance(prev, int) and prev < 2):
                        if isinstance(prev, int):
                            dve.wait_ge(stored[pu % 2][t], 16 * (prev // 2))
                        else:
                            dve.wait_ge(stored[pu % 2][t], prev * 8 - 8 * (pu % 2))
                    wait(dve, out_mm, prev, k + 1, OUT_UNITS)
                    nc.vector.scalar_tensor_tensor(
                        out=RES[:, pu % 2, t, span].rearrange("p (b f) -> p b f", b=2),
                        in0=ps[:, bank:bank + 2, 0:UPIX // 2], scalar=out_bias[:, t:t + 1],
                        in1=X[:, pu, t, span].rearrange("p (b f) -> p b f", b=2),
                        op0=ALU.add, op1=ALU.add).then_inc(result, 1)

                if isinstance(i, int) and i == -1:
                    maximum(0, 1)
                    maximum(0, 0)
                    maximum(0, 2)
                    maximum(1, 0)
                    maximum(1, 1)
                    maximum(1, 2)
                    move_b()
                    q_low(0)
                    q_low(1)
                    stack_low(bottom, slice(CM, P))
                    stack_low(top, slice(0, CM))
                    negate_mean()
                    variance()
                    normalise()
                    gains()
                else:
                    maximum(0, 0)
                    maximum(0, 1)
                    pair_taps()
                    y_low(2, prev, pu)
                    maximum(0, 2)
                    maximum(1, 0)
                    maximum(1, 1)
                    move_b()
                    q_low(0)
                    q_low(1)
                    unit(0)
                    maximum(1, 2)
                    stack_low(bottom, slice(CM, P))
                    negate_mean()
                    unit(1)
                    unit(2)
                    stack_low(top, slice(0, CM))
                    y_low(0)
                    unit(3)
                    unit(4)
                    variance()
                    normalise()
                    unit(5)
                    y_low(1)
                    gains()

            over_images(dve, step)

        @block.tensor
        def _(pe):
            pe.wait_ge(const_in, 16)
            for t in range(HALVES):
                mm = nc.tensor.matmul(pst[:, t:t + 1], wft[0:CM, t, :], bads[0:CM, :], start=True, stop=True)
            mm.then_inc(bias_mm, 1)
            pe.wait_ge(weights_ready, 1)

            def step(i, u):
                j, s, spar = i + 1, i + 2, u % 2
                prev, pu = i - 1, (u - 1) % RING
                def project_f(c):
                    if inside(j):
                        if c == 0:
                            wait(pe, wcn_ready, j, 1)
                            wait(pe, f_evac, i, 1, CHUNKS)
                        elif inside(i - 2):
                            wait(pe, result, i - 2, 5, OUT_UNITS)
                        for t in range(HALVES):
                            for h in range(2):
                                at = HPIX * h + CPIX * c
                                mm = nc.tensor.matmul(ps[CM * h:CM * (h + 1), F_BANKS[c], 0:CPIX],
                                                      wcn_t[:, (u + 1) % 2, t, 0:CM],
                                                      X[:, (u + 1) % RING, t, at:at + CPIX],
                                                      start=(t == 0), stop=(t == HALVES - 1))
                        mm.then_inc(f_mm, 1)

                def unit(k):
                    if not inside(prev):
                        return
                    t, part = divmod(k, UNITS)
                    if k == 0:
                        wait(pe, y_lo, prev, CHUNKS, CHUNKS)
                        if inside(j):
                            wait(pe, f_evac, j, CHUNKS, CHUNKS)
                    wait(pe, result, prev, k - 1, OUT_UNITS)
                    for q in range(2):
                        at = UPIX * part + CPIX * q
                        src = Y[:, pu % 2, at // HPIX, at % HPIX:at % HPIX + CPIX]
                        for w in (wf_hi, wf_lo):
                            mm = nc.tensor.matmul(ps[:, UNIT_BANKS[k % 2] + q, 0:CPIX], w[:, t, :], src,
                                                  start=(w is wf_hi), stop=(w is wf_lo))
                    mm.then_inc(out_mm, 1)

                def conv(slot):
                    if not inside(i):
                        return
                    c, part = divmod(slot, SLOTS)
                    if part == 0:
                        if c == 0:
                            wait(pe, f_stacked, i, 2, 2)
                            wait(pe, q_upper, i, 2, 2)
                            wait(pe, dyn_paired, i, 1)
                        wait(pe, y_lo, i, c - 1, CHUNKS)
                    passes = [(dyn_hi[:, u % 2, tap, :], S, *divmod(tap, K)) for tap in range(TAPS)]
                    passes += [(dyn_lo[:, u % 2, dx, :], Q, 0, dx) for dx in range(K)]
                    passes += [(dyn_lo[:, u % 2, 2 * K + dx, :], S, 2, dx) for dx in range(K)]
                    some = len(passes) // SLOTS
                    for n in range(some * part, some * (part + 1)):
                        w, src, dy, dx = passes[n]
                        for h in range(2):
                            r = HROWS * h + CROWS * c + dy
                            mm = nc.tensor.matmul(
                                ps[CM * h:CM * (h + 1), CONV_BANKS[(CHUNKS * u + c) % 2], 0:CPIX],
                                w, src[:, u % 2, r:r + CROWS, LEFT - 1 + dx:LEFT - 1 + dx + SIDE],
                                start=(n == 0), stop=(n == len(passes) - 1))
                    if part == SLOTS - 1:
                        mm.then_inc(conv_mm, 1)

                def group_mean():
                    if inside(s):
                        wait(pe, means, s, HALVES, HALVES)
                        wait(pe, gains_ready, j, 1)
                        for t in range(HALVES):
                            mm = nc.tensor.matmul(pst[:, 0:1], gavg[:], feats[:, spar, t, MEAN:MEAN + 1],
                                                  start=(t == 0), stop=(t == HALVES - 1))
                        mm.then_inc(gmean_mm, 1)

                def group_var():
                    if inside(s):
                        wait(pe, squares, s, HALVES, HALVES)
                        for t in range(HALVES):
                            mm = nc.tensor.matmul(pst[:, 1:2], gavg[:], sq[:, spar, t:t + 1],
                                                  start=(t == 0), stop=(t == HALVES - 1))
                        mm.then_inc(gvar_mm, 1)

                def project():
                    if inside(s):
                        wait(pe, wcn_ready, s, 1)
                        for t in range(HALVES):
                            mm = nc.tensor.matmul(pst[:, 4:4 + FEATS], wcn_t[:, spar, t, :],
                                                  proj_in[:, spar, t, :],
                                                  start=(t == 0), stop=(t == HALVES - 1))
                        mm.then_inc(proj_mm, 1)

                if isinstance(i, int) and i == -1:
                    group_mean()
                    project_f(0)
                    project_f(1)
                    project_f(2)
                    group_var()
                    project()
                else:
                    project_f(0)
                    project_f(1)
                    project_f(2)
                    conv(0)
                    conv(1)
                    conv(2)
                    conv(3)
                    conv(4)
                    unit(0)
                    unit(1)
                    conv(5)
                    group_mean()
                    conv(6)
                    unit(2)
                    conv(7)
                    conv(8)
                    conv(9)
                    unit(3)
                    unit(4)
                    conv(10)
                    conv(11)
                    group_var()
                    unit(5)
                    conv(12)
                    conv(13)
                    conv(14)
                    project()

            over_images(pe, step)


def kernel(x, L0_conv_Wc, L0_conv_bc, L0_conv_Wkk, L0_conv_bkk, L0_conv_Wck, L0_conv_bck,
           L0_conv_b_ad, L0_conv_Wf, L0_conv_bf):
    import concourse.bacc as bacc
    from concourse.bass_utils import run_bass_kernel_spmd

    x = np.asarray(x)
    n = x.shape[0]

    def twice(a, axis):
        return np.concatenate([np.asarray(a)] * 2, axis)

    def every(a):
        return np.broadcast_to(np.asarray(a).reshape(1, -1), (P, np.size(a)))

    consts = {
        "wc_nat": twice(L0_conv_Wc, 0),
        "wc_t": twice(np.asarray(L0_conv_Wc).T.reshape(P, HALVES, CM), 2),
        "wf_t": twice(np.asarray(L0_conv_Wf).reshape(P, HALVES, CM).transpose(2, 1, 0), 0),
        "bc": twice(L0_conv_bc, 0),
        "b_ad": twice(L0_conv_b_ad, 0),
        "bf": np.asarray(L0_conv_bf),
        "kk": np.concatenate([every(L0_conv_Wkk), every(L0_conv_bkk)], 1),
        "ck": np.concatenate([every(np.asarray(L0_conv_Wck).T), every(L0_conv_bck)], 1),
        "group_avg": np.kron(np.eye(P * HALVES // GROUP), np.full((GROUP // HALVES,) * 2, 1.0 / GROUP))
        .astype(np.float32),
    }
    arrays = {
        "x": x.reshape(n, C, PIX),
        "consts": np.concatenate([consts[name].reshape(P, cols) for name, cols in CONST_COLS.items()], 1),
    }
    nc = bacc.Bacc("TRN2", target_bir_lowering=False, num_devices=1)
    args = [nc.dram_tensor(k, a.shape, mybir.dt.from_np(a.dtype), kind="ExternalInput").ap()
            for k, a in arrays.items()]
    out = nc.dram_tensor("out", (n, C, PIX), F32, kind="ExternalOutput").ap()
    build(nc, *args, out)
    r = run_bass_kernel_spmd(nc, [arrays], core_ids=[0])
    return r.results[0]["out"].reshape(x.shape)
```

```python
from contextlib import ExitStack

import numpy as np

import concourse.bass as bass
import concourse.mybir as mybir
from concourse.alu_op_type import AluOpType as ALU

ACT = mybir.ActivationFunctionType
F32 = mybir.dt.float32
F32R = mybir.dt.float32r
F16 = mybir.dt.float16
I32 = mybir.dt.int32
AX = mybir.AxisListType

P = 128
HALVES = 2
SIDE = 48
PIX = SIDE * SIDE
C = P * HALVES
CM = 64
K = 3
TAPS = K * K
BLOCK = SIDE // K
GROUP = 8
EPS = 1e-5

HROWS = SIDE // 2
HPIX = HROWS * SIDE
CHUNKS = 3
CROWS = HROWS // CHUNKS
CPIX = CROWS * SIDE
LEFT = 2
PITCH = LEFT + SIDE + 2
RING = 6
AHEAD = 4
FIRST, PAST = -3, 2
UNITS = 3
UPIX = PIX // UNITS
SLOTS = 5
AIDED = (1, 4)
MEAN, NEG = TAPS, TAPS + 1
FEATS = TAPS + 2

XN_BOUND = 136.0
F16_SAFE = 30000.0
EXPONENT_BITS = 0x7F800000

BANK = 512
CONV_BANKS = (0, 1)
UNIT_BANKS = (2, 4)
F_BANKS = (6, 2, 3)
STATS_BANK = 7


def count(images, add, per=1):
    return images * per + add


def wait(eng, sem, images, add=0, per=1):
    value = count(images, add, per)
    if not isinstance(value, int) or value > 0:
        eng.wait_ge(sem, value)


CONST_COLS = {
    "wc_nat": C,
    "wc_t": HALVES * P,
    "wf_t": HALVES * P,
    "bc": 1,
    "b_ad": 1,
    "bf": HALVES,
    "kk": 2 * TAPS,
    "ck": 3 * CM,
    "group_avg": P,
}


def build(nc, x, consts, out):
    N = x.shape[0]
    assert N % 2 == 0 and N >= 2 * RING + AHEAD
    ctx = ExitStack()
    with ctx:
        def sb(name, shape, dt=F32):
            return ctx.enter_context(nc.sbuf_tensor(name, shape, dt))

        def sem(name):
            return ctx.enter_context(nc.semaphore(name))

        const = sb("const", [P, sum(CONST_COLS.values())])
        first = dict(zip(CONST_COLS, np.cumsum([0, *CONST_COLS.values()]).tolist()))

        def part(name):
            return const[:, first[name]:first[name] + CONST_COLS[name]]

        wcn, bcs, bads, bfs, gavg = (part(name) for name in ("wc_nat", "bc", "b_ad", "bf", "group_avg"))
        wct = part("wc_t").rearrange("p (t o) -> p t o", t=HALVES)
        wft = part("wf_t").rearrange("p (t o) -> p t o", t=HALVES)
        kk = part("kk").rearrange("p (k l) -> p k l", k=2)
        ck = part("ck").rearrange("p (k o) -> p k o", k=3)
        wf_hi = sb("wf_hi", [P, HALVES, P], F32R)
        wf_lo = sb("wf_lo", [P, HALVES, P], F32R)
        out_bias = sb("out_bias", [P, HALVES])
        bnd = sb("bnd", [P, 16])
        X = sb("X", [P, RING, HALVES, PIX])
        lone = sb("lone", [P, HALVES, UPIX])
        unused = sb("unused", [P, 2, HALVES, PIX], mybir.dt.bfloat16)
        feats = sb("feats", [P, 2, HALVES, FEATS])
        proj_in = sb("proj_in", [P, 2, HALVES, FEATS])
        neg_mean = sb("neg_mean", [P, 2])
        sq = sb("sq", [P, 2, HALVES])
        norm = sb("norm", [P, 2, 5])
        wcn_t = sb("wcn_t", [P, 2, HALVES, P])
        pool_g = sb("pool_g", [P, 2, TAPS])
        mean_act = sb("mean_act", [P, 2, TAPS + 1])
        f_bias = sb("f_bias", [P, 2])
        dyn_a = sb("dyn_a", [P, TAPS, CM])
        dyn_b = sb("dyn_b", [P, TAPS, CM])
        dyn_hi = sb("dyn_hi", [P, 2, TAPS, CM], F16)
        dyn_lo = sb("dyn_lo", [P, 2, TAPS, CM], F16)
        f32 = sb("f32", [P, 2, HROWS, SIDE])
        f_lo = sb("f_lo", [P, 2, HROWS, SIDE], F16)
        S = sb("S", [P, 2, SIDE + 2, PITCH], F16)
        Q = sb("Q", [P, 2, SIDE, PITCH], F16)
        Y = sb("Y", [P, 2, 2, HPIX], F32R)
        Yf = Y[:].bitcast(F32)
        ps = ctx.enter_context(nc.psum_tensor("ps", [P, 8, BANK], F32))
        pst = ps[:, STATS_BANK, :]

        const_in = sem("const_in")
        setup_dve = sem("setup_dve")
        pads_zero = sem("pads_zero")
        bound_all = sem("bound_all")
        bias_mm = sem("bias_mm")
        weights_ready = sem("weights_ready")
        loaded = [[sem(f"loaded_{b}_{t}") for t in range(HALVES)] for b in range(RING)]
        stored = [[sem(f"stored_{b}_{t}") for t in range(HALVES)] for b in range(RING)]
        means = sem("means")
        maxima = sem("maxima")
        gmean_mm = sem("gmean_mm")
        neg_ready = sem("neg_ready")
        squares = sem("squares")
        gvar_mm = sem("gvar_mm")
        var_ready = sem("var_ready")
        feats_read = sem("feats_read")
        std_ready = sem("std_ready")
        norm_step = sem("norm_step")
        wcn_ready = sem("wcn_ready")
        proj_mm = sem("proj_mm")
        relu_ready = sem("relu_ready")
        fbias_ready = sem("fbias_ready")
        gains_ready = sem("gains_ready")
        dyn_step = sem("dyn_step")
        dyn_ready = sem("dyn_ready")
        dyn_paired = sem("dyn_paired")
        f_mm = sem("f_mm")
        f_evac = sem("f_evac")
        flo_ready = sem("flo_ready")
        f_moved = sem("f_moved")
        f_stacked = sem("f_stacked")
        q_filled = sem("q_filled")
        conv_mm = sem("conv_mm")
        y_hi = sem("y_hi")
        y_lo = sem("y_lo")
        out_mm = sem("out_mm")
        result = sem("result")
        evacuated = sem("evacuated")
        added = sem("added")

        xd = x.rearrange("n (p t) f -> n p t f", t=HALVES)
        od = out.rearrange("n (p t) f -> n p t f", t=HALVES)
        DYN_STEPS, NORM_STEPS, OUT_UNITS = 5, 3, HALVES * UNITS
        OUR_UNITS = [k for k in range(OUT_UNITS) if k not in AIDED]

        def over_images(eng, step):
            def at(i, u, lap):
                def im(k):
                    turns, slot = divmod(u + k, RING)
                    return i + k, slot, lap + turns
                return im

            for i in range(FIRST, RING):
                step(at(i, i % RING, i // RING))
            laps = (N - AHEAD) // RING
            with eng.Fori(1, laps) as lap:
                for u in range(RING):
                    step(at(lap * RING + u, u, lap))
            for i in range(RING * laps, N + PAST):
                step(at(i, i % RING, i // RING))

        def inside(i):
            return not isinstance(i, int) or 0 <= i < N

        def wait_loaded(eng, u, lap, t):
            eng.wait_ge(loaded[u][t], (lap + 1) * 16)

        def wait_left(eng, image, k):
            if k in AIDED:
                wait(eng, evacuated, image, AIDED.index(k) + 1, len(AIDED))
            else:
                wait(eng, result, image, OUR_UNITS.index(k) + 1, len(OUR_UNITS))

        def unit_span(k):
            t, part = divmod(k, UNITS)
            return t, slice(UPIX * part, UPIX * (part + 1))

        block = ctx.enter_context(nc.Block())

        @block.sync
        def _(sp):
            sp.dma_start(X[:, 0, 0, :], xd[0, :, 0, :]).then_inc(loaded[0][0], 16)
            sp.dma_start(const[:], consts).then_inc(const_in, 16)
            sp.dma_start(X[:, 0, 1, :], xd[0, :, 1, :]).then_inc(loaded[0][1], 16)

            for b in range(1, AHEAD + 2):
                for t in range(HALVES):
                    sp.dma_start(X[:, b, t, :], xd[b, :, t, :]).then_inc(loaded[b][t], 16)

            def step(im):
                new, slot, turns = im(AHEAD)
                prev, pu, _ = im(-1)
                for t in range(HALVES):
                    if inside(new) and not (isinstance(new, int) and new < RING):
                        sp.wait_ge(stored[slot][t], turns * 16)
                        sp.dma_start(X[:, slot, t, :], xd[new, :, t, :]).then_inc(loaded[slot][t], 16)
                for t in range(HALVES):
                    if inside(prev):
                        sp.wait_ge(added, count(prev, t + 1, HALVES))
                        sp.dma_start(od[prev, :, t, :], X[:, pu, t, :]) \
                            .then_inc(stored[pu][t], 16)

            over_images(sp, step)
            for b in range(RING):
                for t in range(HALVES):
                    sp.wait_ge(stored[b][t], 16 * len(range(b, N, RING)))

        @block.gpsimd
        def _(pool):
            nc.gpsimd.memset(feats[:], 0.0).then_inc(pads_zero, 1)
            nc.gpsimd.memset(S[:], 0.0).then_inc(pads_zero, 1)
            nc.gpsimd.memset(Q[:], 0.0).then_inc(pads_zero, 1)
            pool.wait_ge(setup_dve, 3)
            nc.gpsimd.partition_all_reduce(bnd[:, 2:3], bnd[:, 1:2], P, bass.bass_isa.ReduceOp.max) \
                .then_inc(bound_all, 1)
            pool.wait_ge(weights_ready, 1)

            def step(im):
                def weight_terms(image):
                    n, u, lap = image
                    if not inside(n):
                        return
                    pool.wait_ge(gains_ready, count(n, 1))
                    wait(pool, dyn_ready, n, 0, 2)
                    w0 = ck[:, 0:1, :].to_broadcast([P, TAPS, CM])
                    w1 = ck[:, 1:2, :].to_broadcast([P, TAPS, CM])
                    g = pool_g[:, u % 2, :].unsqueeze(2).to_broadcast([P, TAPS, CM])
                    s = mean_act[:, u % 2, 0:TAPS].unsqueeze(2).to_broadcast([P, TAPS, CM])
                    nc.gpsimd.tensor_tensor(dyn_a[:], w0, g, ALU.mult).then_inc(dyn_step, 1)
                    nc.gpsimd.tensor_tensor(dyn_b[:], w1, s, ALU.mult).then_inc(dyn_step, 1)

                def weight_sum(image):
                    n, u, lap = image
                    if inside(n):
                        b0 = ck[:, 2:3, :].to_broadcast([P, TAPS, CM])
                        pool.wait_ge(dyn_step, count(n, 2, DYN_STEPS))
                        nc.gpsimd.tensor_tensor(dyn_a[:], dyn_a[:], dyn_b[:], ALU.add).then_inc(dyn_step, 1)
                        pool.wait_ge(dyn_step, count(n, 3, DYN_STEPS))
                        nc.gpsimd.tensor_tensor(dyn_a[:], dyn_a[:], b0, ALU.add).then_inc(dyn_step, 1)

                def f_low_and_relu(image):
                    n, u, lap = image
                    if inside(n):
                        pool.wait_ge(dyn_step, count(n, 4, DYN_STEPS))
                        pool.wait_ge(f_evac, count(n, CHUNKS, CHUNKS))
                        nc.gpsimd.tensor_tensor(f_lo[:, u % 2], f32[:, u % 2],
                                                S[:, u % 2, 1:1 + HROWS, LEFT:LEFT + SIDE], ALU.subtract) \
                            .then_inc(flo_ready, 1)
                        nc.gpsimd.tensor_scalar(dyn_b[:], dyn_a[:], 0.0, None, ALU.max).then_inc(dyn_step, 1)
                        nc.gpsimd.tensor_scalar(dyn_hi[:, u % 2], dyn_a[:], 0.0, None, ALU.max) \
                            .then_inc(dyn_ready, 1)

                def weight_low(image):
                    n, u, lap = image
                    if inside(n):
                        pool.wait_ge(dyn_step, count(n, 5, DYN_STEPS))
                        pool.wait_ge(dyn_ready, count(n, 1, 2))
                        nc.gpsimd.tensor_tensor(dyn_lo[:, u % 2], dyn_b[:], dyn_hi[:, u % 2], ALU.subtract) \
                            .then_inc(dyn_ready, 1)

                def add_x(k, image):
                    n, u, lap = image
                    if inside(n):
                        t, span = unit_span(k)
                        pool.wait_ge(evacuated, count(n, t + 1, HALVES))
                        pool.wait_ge(result, count(n, sum(k < UNITS * (t + 1) for k in OUR_UNITS), len(OUR_UNITS)))
                        nc.gpsimd.tensor_tensor(X[:, u, t, span], X[:, u, t, span], lone[:, t, :],
                                                ALU.add).then_inc(added, 1)

                f_low_and_relu(im(1))
                weight_low(im(1))
                add_x(1, im(-1))
                add_x(4, im(-1))
                weight_terms(im(2))
                weight_sum(im(2))

            over_images(pool, step)

        @block.scalar
        def _(act):
            act.wait_ge(pads_zero, 1)

            def step(im):
                def f_out(c, image):
                    n, u, lap = image
                    if not inside(n):
                        return
                    src = ps[:, F_BANKS[c], 0:CPIX].rearrange("p (r w) -> p r w", w=SIDE)
                    if c == 0:
                        act.wait_ge(fbias_ready, count(n, 1))
                        if isinstance(n, int) and n == 0:
                            act.wait_ge(pads_zero, 3)
                    act.wait_ge(f_mm, count(n, c + 1, CHUNKS))
                    nc.scalar.activation(S[:, u % 2, 1 + CROWS * c:1 + CROWS * (c + 1), LEFT:LEFT + SIDE],
                                         src, ACT.Relu, bias=f_bias[:, u % 2:u % 2 + 1])
                    nc.scalar.activation(f32[:, u % 2, CROWS * c:CROWS * (c + 1), :], src, ACT.Relu,
                                         bias=f_bias[:, u % 2:u % 2 + 1]).then_inc(f_evac, 1)

                def channel_means(t, image):
                    n, u, lap = image
                    if inside(n):
                        wait_loaded(act, u, lap, t)
                        wait(act, means, n, t - 1, HALVES)
                        if t == 0:
                            wait(act, feats_read, n, -1)
                        nc.scalar.activation(unused[:, 0, t], X[:, u, t, :], ACT.Identity,
                                             scale=1.0 / PIX, accum_out=feats[:, u % 2, t, MEAN:MEAN + 1]) \
                            .then_inc(means, 1)

                def square_sum(t, image):
                    n, u, lap = image
                    if inside(n):
                        if t == 0:
                            act.wait_ge(neg_ready, count(n, 1))
                        wait(act, squares, n, t - 1, HALVES)
                        nc.scalar.activation(unused[:, 1, t], X[:, u, t, :], ACT.Square,
                                             bias=neg_mean[:, u % 2:u % 2 + 1],
                                             accum_out=sq[:, u % 2, t:t + 1]).then_inc(squares, 1)

                def deviation(image):
                    n, u, lap = image
                    if inside(n):
                        act.wait_ge(var_ready, count(n, 1))
                        nc.scalar.activation(norm[:, u % 2, 1:2], norm[:, u % 2, 0:1], ACT.Sqrt) \
                            .then_inc(std_ready, 1)

                def unit(k, image):
                    n, u, lap = image
                    if inside(n):
                        t, span = unit_span(k)
                        wait(act, added, n, t - 1, HALVES)
                        act.wait_ge(out_mm, count(n, k + 1, OUT_UNITS))
                        bank = UNIT_BANKS[k % 2]
                        nc.scalar.activation(lone[:, t, :].rearrange("p (b f) -> p b f", b=2),
                                             ps[:, bank:bank + 2, 0:UPIX // 2], ACT.Identity,
                                             bias=out_bias[:, t:t + 1]).then_inc(evacuated, 1)

                def y_high(c, image):
                    n, u, lap = image
                    if not inside(n):
                        return
                    act.wait_ge(conv_mm, count(n, c + 1, CHUNKS))
                    for h in range(2):
                        lanes = slice(CM * h, CM * (h + 1))
                        nc.scalar.activation(Y[lanes, u % 2, h, CPIX * c:CPIX * (c + 1)],
                                             ps[lanes, CONV_BANKS[(CHUNKS * u + c) % 2], 0:CPIX],
                                             ACT.Copy).then_inc(y_hi, 1)

                y_high(2, im(-1))
                f_out(0, im(1))
                f_out(1, im(1))
                f_out(2, im(1))
                channel_means(1, im(2))
                y_high(0, im(0))
                unit(1, im(-1))
                square_sum(0, im(2))
                square_sum(1, im(2))
                unit(4, im(-1))
                deviation(im(2))
                y_high(1, im(0))
                channel_means(0, im(3))

            over_images(act, step)

        @block.vector
        def _(dve):
            done = [0]

            def link(ins):
                done[0] += 1
                ins.then_inc(setup_dve, 1)
                dve.wait_ge(setup_dve, done[0])

            def pow2_below(col):
                c = bnd[:, col:col + 1].bitcast(I32)
                link(nc.vector.tensor_scalar(c, c, EXPONENT_BITS, None, ALU.bitwise_and))

            dve.wait_ge(const_in, 16)
            dve.wait_ge(pads_zero, 1)
            link(nc.vector.tensor_reduce(bnd[:, 0:1], wcn[:], AX.X, ALU.add, apply_absolute_value=True))
            link(nc.vector.tensor_reduce(bnd[:, 15:16], bcs[:], AX.X, ALU.add, apply_absolute_value=True))
            link(nc.vector.scalar_tensor_tensor(out=bnd[:, 1:2], in0=bnd[:, 0:1], scalar=XN_BOUND,
                                                in1=bnd[:, 15:16], op0=ALU.mult, op1=ALU.add))
            dve.wait_ge(bound_all, 1)
            link(nc.vector.tensor_scalar(bnd[:, 3:4], bnd[:, 2:3], 1e-20, 1.0 / F16_SAFE, ALU.max, ALU.mult))
            link(nc.vector.reciprocal(bnd[:, 4:5], bnd[:, 3:4]))
            pow2_below(4)
            link(nc.vector.reciprocal(bnd[:, 5:6], bnd[:, 4:5]))
            link(nc.vector.tensor_reduce(bnd[:, 6:8], kk[:], AX.X, ALU.max, apply_absolute_value=True))
            link(nc.vector.tensor_reduce(bnd[:, 8:11], ck[:], AX.X, ALU.max, apply_absolute_value=True))
            link(nc.vector.scalar_tensor_tensor(out=bnd[:, 11:12], in0=bnd[:, 2:3], scalar=bnd[:, 6:7],
                                                in1=bnd[:, 7:8], op0=ALU.mult, op1=ALU.add))
            link(nc.vector.scalar_tensor_tensor(out=bnd[:, 11:12], in0=bnd[:, 11:12], scalar=bnd[:, 8:9],
                                                in1=bnd[:, 10:11], op0=ALU.mult, op1=ALU.add))
            link(nc.vector.scalar_tensor_tensor(out=bnd[:, 11:12], in0=bnd[:, 2:3], scalar=bnd[:, 9:10],
                                                in1=bnd[:, 11:12], op0=ALU.mult, op1=ALU.add))
            link(nc.vector.tensor_scalar(bnd[:, 11:12], bnd[:, 11:12], 1e-20, 1.0 / F16_SAFE, ALU.max, ALU.mult))
            link(nc.vector.reciprocal(bnd[:, 12:13], bnd[:, 11:12]))
            pow2_below(12)
            link(nc.vector.reciprocal(bnd[:, 13:14], bnd[:, 12:13]))
            dve.wait_ge(bias_mm, 1)
            link(nc.vector.tensor_tensor(out_bias[:], pst[:, 0:HALVES], bfs[:], ALU.add))
            link(nc.vector.tensor_scalar(wft[:], wft[:], bnd[:, 5:6], bnd[:, 13:14], ALU.mult, ALU.mult))
            link(nc.vector.tensor_copy(wf_hi[:], wft[:]))
            link(nc.vector.tensor_tensor(wf_lo[:], wft[:], wf_hi[:].bitcast(F32), ALU.subtract))
            link(nc.vector.tensor_scalar(wct[:], wct[:], bnd[:, 4:5], None, ALU.mult))
            link(nc.vector.tensor_scalar(bcs[:], bcs[:], bnd[:, 4:5], None, ALU.mult))
            link(nc.vector.tensor_scalar(kk[:, 0, :], kk[:, 0, :], bnd[:, 5:6], None, ALU.mult))
            link(nc.vector.tensor_scalar(ck[:], ck[:], bnd[:, 12:13], None, ALU.mult))
            link(nc.vector.tensor_scalar(ck[:, 1, :], ck[:, 1, :], bnd[:, 5:6], None, ALU.mult))
            nc.vector.memset(bnd[:, 14:15], 1.0).then_inc(weights_ready, 1)

            def step(im):
                top, bottom = slice(1, 1 + HROWS), slice(1 + HROWS, 1 + SIDE)
                cols = slice(LEFT, LEFT + SIDE)

                def y_low(c, image):
                    n, u, lap = image
                    if not inside(n):
                        return
                    for h in range(2):
                        src, dst = slice(CM * h, CM * (h + 1)), slice(CM * (1 - h), CM * (2 - h))
                        dve.wait_ge(y_hi, count(n, 2 * c + h + 1, 2 * CHUNKS))
                        ins = nc.vector.tensor_tensor(Y[dst, u % 2, h, CPIX * c:CPIX * (c + 1)],
                                                      ps[src, CONV_BANKS[(CHUNKS * u + c) % 2], 0:CPIX],
                                                      Yf[src, u % 2, h, CPIX * c:CPIX * (c + 1)], ALU.subtract)
                    ins.then_inc(y_lo, 1)

                def pair_taps(image):
                    n, u, lap = image
                    if inside(n):
                        dve.wait_ge(dyn_ready, count(n, 2, 2))
                        nc.vector.tensor_copy(dyn_lo[CM:P, u % 2, 0:K], dyn_lo[CM:P, u % 2, K:2 * K]) \
                            .then_inc(dyn_paired, 1)

                def maximum(t, k, image):
                    n, u, lap = image
                    if inside(n):
                        wait_loaded(dve, u, lap, t)
                        rows = slice(BLOCK * SIDE * k, BLOCK * SIDE * (k + 1))
                        nc.vector.tensor_reduce(
                            feats[:, u % 2, t, K * k:K * (k + 1)],
                            X[:, u, t, rows].rearrange("p (h l w) -> p l h w", h=BLOCK, l=K),
                            AX.XY, ALU.max).then_inc(maxima, 1)

                def move_b(image):
                    n, u, lap = image
                    if inside(n):
                        dve.wait_ge(f_evac, count(n, CHUNKS, CHUNKS))
                        nc.vector.tensor_copy(S[0:CM, u % 2, bottom, cols], S[CM:P, u % 2, top, cols]) \
                            .then_inc(f_moved, 1)

                def q_low(h, image):
                    n, u, lap = image
                    if inside(n):
                        if isinstance(n, int) and n == 0:
                            dve.wait_ge(pads_zero, 3)
                        if h == 0:
                            dve.wait_ge(f_evac, count(n, CHUNKS, CHUNKS))
                        else:
                            dve.wait_ge(f_moved, count(n, 1))
                        rows = slice(1, 1 + HROWS) if h == 0 else slice(1 + HROWS, SIDE)
                        nc.vector.tensor_copy(Q[0:CM, u % 2, rows, :], S[0:CM, u % 2, rows, :]) \
                            .then_inc(q_filled, 1)

                def q_up(h, image):
                    n, u, lap = image
                    if inside(n):
                        dve.wait_ge(f_moved, count(n, 1))
                        nc.vector.tensor_copy(Q[CM:P, u % 2, HROWS * h:HROWS * (h + 1), cols],
                                              S[0:CM, u % 2, 1 + HROWS * h:1 + HROWS * (h + 1), cols]) \
                            .then_inc(q_filled, 1)

                def stack_low(rows, lanes, image):
                    n, u, lap = image
                    if inside(n):
                        dve.wait_ge(flo_ready, count(n, 1))
                        dve.wait_ge(f_moved, count(n, 1))
                        nc.vector.tensor_copy(S[CM:P, u % 2, rows, cols], f_lo[lanes, u % 2]).then_inc(f_stacked, 1)

                def negate_mean(image):
                    n, u, lap = image
                    if inside(n):
                        dve.wait_ge(gmean_mm, count(n, 1))
                        wait(dve, squares, n, -HALVES, HALVES)
                        nc.vector.tensor_scalar(neg_mean[:, u % 2:u % 2 + 1], pst[:, 0:1], -1.0, None, ALU.mult) \
                            .then_inc(neg_ready, 1)

                def variance(image):
                    n, u, lap = image
                    if inside(n):
                        dve.wait_ge(gvar_mm, count(n, 1))
                        nc.vector.tensor_scalar(norm[:, u % 2, 0:1], pst[:, 1:2], 1.0 / PIX, EPS, ALU.mult, ALU.add) \
                            .then_inc(var_ready, 1)
                        dve.wait_ge(neg_ready, count(n, 1))
                        dve.wait_ge(maxima, count(n, HALVES * K, HALVES * K))
                        dve.wait_ge(means, count(n, HALVES, HALVES))
                        nc.vector.tensor_scalar(proj_in[:, u % 2], feats[:, u % 2], neg_mean[:, u % 2:u % 2 + 1],
                                                None, ALU.add).then_inc(feats_read, 1)

                def normalise(image):
                    n, u, lap = image
                    if inside(n):
                        dve.wait_ge(std_ready, count(n, 1))
                        var, std, r0, e, half = (norm[:, u % 2, q:q + 1] for q in range(5))
                        nc.vector.reciprocal(r0, std).then_inc(norm_step, 1)
                        dve.wait_ge(norm_step, count(n, 1, NORM_STEPS))
                        nc.vector.scalar_tensor_tensor(out=e, in0=r0, scalar=var, in1=r0,
                                                       op0=ALU.mult, op1=ALU.mult).then_inc(norm_step, 1)
                        dve.wait_ge(norm_step, count(n, 2, NORM_STEPS))
                        nc.vector.tensor_scalar(half, e, -0.5, 1.5, ALU.mult, ALU.add).then_inc(norm_step, 1)
                        dve.wait_ge(norm_step, count(n, 3, NORM_STEPS))
                        wait(dve, f_mm, n, -CHUNKS, CHUNKS)
                        nc.vector.tensor_scalar(wcn_t[:, u % 2], wct[:], r0, half, ALU.mult, ALU.mult) \
                            .then_inc(wcn_ready, 1)

                def gains(image):
                    n, u, lap = image
                    if inside(n):
                        dve.wait_ge(proj_mm, count(n, 1))
                        wait(dve, f_evac, n, -CHUNKS, CHUNKS)
                        wait(dve, dyn_step, n, 2 - 2 * DYN_STEPS, DYN_STEPS)
                        nc.vector.tensor_scalar(f_bias[:, u % 2:u % 2 + 1], pst[:, 4 + NEG:5 + NEG], bcs[:], None,
                                                ALU.add).then_inc(fbias_ready, 1)
                        nc.vector.tensor_scalar(mean_act[:, u % 2], pst[:, 4:4 + TAPS + 1], bcs[:], 0.0,
                                                ALU.add, ALU.max).then_inc(relu_ready, 1)
                        dve.wait_ge(relu_ready, count(n, 1))
                        nc.vector.scalar_tensor_tensor(out=pool_g[:, u % 2, :], in0=kk[:, 0, :],
                                                       scalar=mean_act[:, u % 2, MEAN:MEAN + 1],
                                                       in1=kk[:, 1, :], op0=ALU.mult, op1=ALU.add) \
                            .then_inc(gains_ready, 1)

                def unit(k, image):
                    n, u, lap = image
                    if not inside(n):
                        return
                    t, span = unit_span(k)
                    bank = UNIT_BANKS[k % 2]
                    dve.wait_ge(out_mm, count(n, k + 1, OUT_UNITS))
                    nc.vector.scalar_tensor_tensor(
                        out=X[:, u, t, span].rearrange("p (b f) -> p b f", b=2),
                        in0=ps[:, bank:bank + 2, 0:UPIX // 2], scalar=out_bias[:, t:t + 1],
                        in1=X[:, u, t, span].rearrange("p (b f) -> p b f", b=2),
                        op0=ALU.add, op1=ALU.add).then_inc(result, 1)

                unit(5, im(-2))
                gains(im(1))
                maximum(1, 0, im(2))
                maximum(1, 2, im(2))
                y_low(2, im(-1))
                maximum(0, 2, im(2))
                move_b(im(1))
                q_low(0, im(1))
                q_low(1, im(1))
                unit(0, im(-1))
                negate_mean(im(2))
                maximum(0, 0, im(3))
                unit(2, im(-1))
                q_up(1, im(1))
                stack_low(top, slice(0, CM), im(1))
                y_low(0, im(0))
                unit(3, im(-1))
                maximum(0, 1, im(3))
                q_up(0, im(1))
                variance(im(2))
                normalise(im(2))
                y_low(1, im(0))
                maximum(1, 1, im(3))
                pair_taps(im(1))
                stack_low(bottom, slice(CM, P), im(1))

            over_images(dve, step)

        @block.tensor
        def _(pe):
            pe.wait_ge(const_in, 16)
            for t in range(HALVES):
                mm = nc.tensor.matmul(pst[:, t:t + 1], wft[0:CM, t, :], bads[0:CM, :], start=True, stop=True)
            mm.then_inc(bias_mm, 1)
            pe.wait_ge(weights_ready, 1)

            def step(im):
                def project_f(c, image):
                    n, u, lap = image
                    if inside(n):
                        if c == 0:
                            pe.wait_ge(wcn_ready, count(n, 1))
                            wait(pe, f_evac, n - 1, 1, CHUNKS)
                        elif inside(n - 3):
                            wait_left(pe, n - 3, OUT_UNITS - 2)
                        for t in range(HALVES):
                            for h in range(2):
                                at = HPIX * h + CPIX * c
                                mm = nc.tensor.matmul(ps[CM * h:CM * (h + 1), F_BANKS[c], 0:CPIX],
                                                      wcn_t[:, u % 2, t, 0:CM],
                                                      X[:, u, t, at:at + CPIX],
                                                      start=(t == 0), stop=(t == HALVES - 1))
                        mm.then_inc(f_mm, 1)

                def unit(k, image):
                    n, u, lap = image
                    if not inside(n):
                        return
                    t, part = divmod(k, UNITS)
                    if k == 0:
                        pe.wait_ge(y_lo, count(n, CHUNKS, CHUNKS))
                        if inside(n + 2):
                            wait(pe, f_evac, n + 2, CHUNKS, CHUNKS)
                    if k >= 2:
                        wait_left(pe, n, k - 2)
                    elif inside(n - 1):
                        wait_left(pe, n - 1, OUT_UNITS - 2 + k)
                    for q in range(2):
                        at = UPIX * part + CPIX * q
                        src = Y[:, u % 2, at // HPIX, at % HPIX:at % HPIX + CPIX]
                        for w in (wf_hi, wf_lo):
                            mm = nc.tensor.matmul(ps[:, UNIT_BANKS[k % 2] + q, 0:CPIX], w[:, t, :], src,
                                                  start=(w is wf_hi), stop=(w is wf_lo))
                    mm.then_inc(out_mm, 1)

                def conv(slot, image):
                    n, u, lap = image
                    if not inside(n):
                        return
                    c, part = divmod(slot, SLOTS)
                    if part == 0:
                        if c == 0:
                            pe.wait_ge(f_stacked, count(n, 2, 2))
                            pe.wait_ge(q_filled, count(n, 4, 4))
                            pe.wait_ge(dyn_paired, count(n, 1))
                        wait(pe, y_lo, n, c - 1, CHUNKS)
                    passes = [(dyn_hi[:, u % 2, tap, :], S, *divmod(tap, K)) for tap in range(TAPS)]
                    passes += [(dyn_lo[:, u % 2, dx, :], Q, 0, dx) for dx in range(K)]
                    passes += [(dyn_lo[:, u % 2, 2 * K + dx, :], S, 2, dx) for dx in range(K)]
                    some = len(passes) // SLOTS
                    for n in range(some * part, some * (part + 1)):
                        w, src, dy, dx = passes[n]
                        for h in range(2):
                            r = HROWS * h + CROWS * c + dy
                            mm = nc.tensor.matmul(
                                ps[CM * h:CM * (h + 1), CONV_BANKS[(CHUNKS * u + c) % 2], 0:CPIX],
                                w, src[:, u % 2, r:r + CROWS, LEFT - 1 + dx:LEFT - 1 + dx + SIDE],
                                start=(n == 0), stop=(n == len(passes) - 1))
                    if part == SLOTS - 1:
                        mm.then_inc(conv_mm, 1)

                def group_mean(image):
                    n, u, lap = image
                    if inside(n):
                        pe.wait_ge(means, count(n, HALVES, HALVES))
                        wait(pe, gains_ready, n - 1, 1)
                        for t in range(HALVES):
                            mm = nc.tensor.matmul(pst[:, 0:1], gavg[:], feats[:, u % 2, t, MEAN:MEAN + 1],
                                                  start=(t == 0), stop=(t == HALVES - 1))
                        mm.then_inc(gmean_mm, 1)

                def group_var(image):
                    n, u, lap = image
                    if inside(n):
                        pe.wait_ge(squares, count(n, HALVES, HALVES))
                        for t in range(HALVES):
                            mm = nc.tensor.matmul(pst[:, 1:2], gavg[:], sq[:, u % 2, t:t + 1],
                                                  start=(t == 0), stop=(t == HALVES - 1))
                        mm.then_inc(gvar_mm, 1)

                def project(image):
                    n, u, lap = image
                    if inside(n):
                        pe.wait_ge(wcn_ready, count(n, 1))
                        for t in range(HALVES):
                            mm = nc.tensor.matmul(pst[:, 4:4 + FEATS], wcn_t[:, u % 2, t, :],
                                                  proj_in[:, u % 2, t, :],
                                                  start=(t == 0), stop=(t == HALVES - 1))
                        mm.then_inc(proj_mm, 1)

                project_f(0, im(1))
                project_f(1, im(1))
                project_f(2, im(1))
                conv(0, im(0))
                conv(1, im(0))
                conv(2, im(0))
                conv(3, im(0))
                conv(4, im(0))
                conv(5, im(0))
                unit(0, im(-1))
                unit(1, im(-1))
                group_mean(im(2))
                conv(6, im(0))
                unit(2, im(-1))
                unit(3, im(-1))
                conv(7, im(0))
                conv(8, im(0))
                unit(4, im(-1))
                conv(9, im(0))
                conv(10, im(0))
                conv(11, im(0))
                group_var(im(2))
                unit(5, im(-1))
                conv(12, im(0))
                conv(13, im(0))
                conv(14, im(0))
                project(im(2))

            over_images(pe, step)


def kernel(x, L0_conv_Wc, L0_conv_bc, L0_conv_Wkk, L0_conv_bkk, L0_conv_Wck, L0_conv_bck,
           L0_conv_b_ad, L0_conv_Wf, L0_conv_bf):
    import concourse.bacc as bacc
    from concourse.bass_utils import run_bass_kernel_spmd

    x = np.asarray(x)
    n = x.shape[0]

    def twice(a, axis):
        return np.concatenate([np.asarray(a)] * 2, axis)

    def every(a):
        return np.broadcast_to(np.asarray(a).reshape(1, -1), (P, np.size(a)))

    consts = {
        "wc_nat": twice(L0_conv_Wc, 0),
        "wc_t": twice(np.asarray(L0_conv_Wc).T.reshape(P, HALVES, CM), 2),
        "wf_t": twice(np.asarray(L0_conv_Wf).reshape(P, HALVES, CM).transpose(2, 1, 0), 0),
        "bc": twice(L0_conv_bc, 0),
        "b_ad": twice(L0_conv_b_ad, 0),
        "bf": np.asarray(L0_conv_bf),
        "kk": np.concatenate([every(L0_conv_Wkk), every(L0_conv_bkk)], 1),
        "ck": np.concatenate([every(np.asarray(L0_conv_Wck).T), every(L0_conv_bck)], 1),
        "group_avg": np.kron(np.eye(P * HALVES // GROUP), np.full((GROUP // HALVES,) * 2, 1.0 / GROUP))
        .astype(np.float32),
    }
    arrays = {
        "x": x.reshape(n, C, PIX),
        "consts": np.concatenate([consts[name].reshape(P, cols) for name, cols in CONST_COLS.items()], 1),
    }
    nc = bacc.Bacc("TRN2", target_bir_lowering=False, num_devices=1)
    args = [nc.dram_tensor(k, a.shape, mybir.dt.from_np(a.dtype), kind="ExternalInput").ap()
            for k, a in arrays.items()]
    out = nc.dram_tensor("out", (n, C, PIX), F32, kind="ExternalOutput").ap()
    build(nc, *args, out)
    r = run_bass_kernel_spmd(nc, [arrays], core_ids=[0])
    return r.results[0]["out"].reshape(x.shape)
```
